# Optimizing a Trainium2 kernel written in Bass

```python
import numpy as np
import jax
import jax.numpy as jnp

def _softmax(x, axis=-1):
    return jax.nn.softmax(x, axis=axis)

def _gelu(x):
    return jax.nn.gelu(x, approximate=True)

def _silu(x):
    return jax.nn.silu(x)

def _sigmoid(x):
    return jax.nn.sigmoid(x)

def _layernorm(x, axis=-1, eps=1e-05):
    m = jnp.mean(x, axis=axis, keepdims=True)
    v = jnp.var(x, axis=axis, keepdims=True)
    return (x - m) / jnp.sqrt(v + eps)

def _scatter_add(tgt, idx, src, axis=0):
    return tgt.at[idx].add(src)

def _segment_sum(src, seg, n):
    return jax.ops.segment_sum(src, seg, n)
kernel_name = 'mk_decoder_preln_d1_seqx_r8_7f2920'

def setup_inputs(seed: int=0):
    np.random.seed(seed)
    _w = jnp.asarray

    def _rec_inputs():
        import jax
        import jax.numpy as jnp
        _rk = jax.random.key(seed)
        x = -0.0005207 + 1.001 * jax.random.normal(jax.random.fold_in(_rk, 1), (2, 512, 128), jnp.float32)
        _lenS = 512 - jax.random.randint(jax.random.fold_in(_rk, 7), (2,), 0, max(1, 512 // 4) + 1, jnp.int32)
        _lenS2 = 77 - jax.random.randint(jax.random.fold_in(_rk, 8), (2,), 0, max(1, 77 // 4) + 1, jnp.int32)
        _ctx_1024P = jax.random.normal(jax.random.fold_in(_rk, 12), (2, 16, 128), jnp.float32)
        _ctx_1024c = jax.random.dirichlet(jax.random.fold_in(_rk, 512), 0.3 * jnp.ones((16,), jnp.float32), (2, 77))
        _ctx_1024t = jnp.einsum('bsk,bkd->bsd', _ctx_1024c, _ctx_1024P)
        _ctx_1024t = _ctx_1024t * jax.lax.rsqrt(jnp.mean(jnp.square(_ctx_1024t)) + 1e-12) * 0.953939
        ctx_1024 = 0.00191187 + 0.999416 * (_ctx_1024t + 0.3 * jax.random.normal(jax.random.fold_in(_rk, 612), (2, 77, 128), jnp.float32))
        _validS = jnp.arange(512)[None, :] < _lenS[:, None]
        _validS2 = jnp.arange(77)[None, :] < _lenS2[:, None]
        _causal = jnp.tril(jnp.ones((512, 512), dtype=bool))
        mask_BxS_ff1 = jnp.where(jnp.ones((2, 512), dtype=bool), 1.0, 0.0).astype(jnp.float32)
        mask_BxS2_ik0 = jnp.where(jnp.broadcast_to(_validS2[:, :], (2, 77)), 0, 1).astype(jnp.int32)
        return (x, ctx_1024, mask_BxS_ff1, mask_BxS2_ik0)
    x, ctx_1024, mask_BxS_ff1, mask_BxS2_ik0 = _rec_inputs()

    def _L0_attn_setup():
        import jax, jax.numpy as jnp
        import numpy as np
        B, L, D = (8, 512, 128)
        LN_EPS = 1e-05

        def _linear_attn(q, k, v):
            d = q.shape[-1]
            q = jax.nn.softmax(q, axis=-1) * d ** (-0.5)
            k = jax.nn.softmax(k, axis=-2)
            context = jnp.einsum('bld,ble->bde', k, v)
            return jnp.einsum('bld,bde->ble', q, context)

        def _layernorm(x, gamma, beta):
            mu = jnp.mean(x, axis=-1, keepdims=True)
            var = jnp.var(x, axis=-1, keepdims=True)
            return (x - mu) * jax.lax.rsqrt(var + LN_EPS) * gamma + beta
        key = jax.random.key(seed)
        ks = jax.random.split(key, 5)
        scale = 1.0 / np.sqrt(D)
        return {'x': jax.random.normal(ks[0], (B, L, D), dtype=jnp.float32), 'Wq': jax.random.normal(ks[1], (D, D), dtype=jnp.float32) * scale, 'Wk': jax.random.normal(ks[2], (D, D), dtype=jnp.float32) * scale, 'Wv': jax.random.normal(ks[3], (D, D), dtype=jnp.float32) * scale, 'Wo': jax.random.normal(ks[4], (D, D), dtype=jnp.float32) * scale, 'bo': jnp.zeros((D,), dtype=jnp.float32), 'gamma': jnp.ones((D,), dtype=jnp.float32), 'beta': jnp.zeros((D,), dtype=jnp.float32)}
    _L0_attn_all = _L0_attn_setup()
    _L0_attn_in = {k: v for k, v in _L0_attn_all.items() if k in ('Wq', 'Wk', 'Wv', 'Wo', 'bo', 'gamma', 'beta')}
    del _L0_attn_all

    def _L0_xattn_setup():
        import jax, jax.numpy as jnp
        import numpy as np
        B, F, T, D = (8, 32, 32, 128)
        NEG = -1e+30
        key = jax.random.key(seed)
        ks = jax.random.split(key, 10)
        s = 1.0 / np.sqrt(D)
        return {'features': jax.random.normal(ks[0], (B, F, D), jnp.float32), 'masks': jnp.ones((B, F), jnp.float32), 'textual_features': jax.random.normal(ks[1], (B, T, D), jnp.float32), 'q_masks': jax.random.randint(ks[2], (B, T), 0, 2, jnp.int32), 'Ws': jax.random.normal(ks[3], (D, D), jnp.float32) * s, 'W': jax.random.normal(ks[4], (D, D), jnp.float32) * s, 'w': jax.random.normal(ks[5], (D, 1), jnp.float32) * s, 'b': jax.random.normal(ks[6], (1, D), jnp.float32) * s, 'Wcw': jax.random.normal(ks[7], (1, D), jnp.float32) * s, 'bcw': jnp.zeros((1,), jnp.float32), 'Wcb': jax.random.normal(ks[8], (1, D), jnp.float32) * s, 'bcb': jnp.zeros((1,), jnp.float32)}
    _L0_xattn_all = _L0_xattn_setup()
    _L0_xattn_in = {k: v for k, v in _L0_xattn_all.items() if k in ('Ws', 'W', 'w', 'b', 'Wcw', 'bcw', 'Wcb', 'bcb')}
    del _L0_xattn_all

    def _L0_ffn_setup():
        import jax, jax.numpy as jnp
        import numpy as np
        B, S, H = (2, 128, 128)
        DFF = 256
        E = 8
        TOPK = 2

        def _expert_ffn(x, w1, b1, w2, b2, wg, bg, w3, b3):
            x1 = jnp.einsum('bsh,hf->bsf', x, w1) + b1
            x2 = jnp.einsum('bsh,hf->bsf', x, w2) + b2
            z = x1 * x2
            s = jax.nn.silu(jnp.einsum('bsf,fg->bsg', z, wg) + bg)
            return jnp.einsum('bsg,gh->bsh', s, w3) + b3
        key = jax.random.key(seed)
        ks = jax.random.split(key, 12)
        sc = 0.02
        return {'x': jax.random.normal(ks[0], (B, S, H), jnp.float32), 'gate_w': jax.random.normal(ks[1], (H, E), jnp.float32) * sc, 'gate_b': jnp.zeros((E,), jnp.float32), 'w1': jax.random.normal(ks[2], (E, H, DFF), jnp.float32) * sc, 'b1': jnp.zeros((E, DFF), jnp.float32), 'w2': jax.random.normal(ks[3], (E, H, DFF), jnp.float32) * sc, 'b2': jnp.zeros((E, DFF), jnp.float32), 'wg': jax.random.normal(ks[4], (E, DFF, DFF), jnp.float32) * sc, 'bg': jnp.zeros((E, DFF), jnp.float32), 'w3': jax.random.normal(ks[5], (E, DFF, H), jnp.float32) * sc, 'b3': jnp.zeros((E, H), jnp.float32)}
    _L0_ffn_all = _L0_ffn_setup()
    _L0_ffn_in = {k: v for k, v in _L0_ffn_all.items() if k in ('gate_w', 'gate_b', 'w1', 'b1', 'w2', 'b2', 'wg', 'bg', 'w3', 'b3')}
    del _L0_ffn_all
    return {'x': x, 'ctx_1024': ctx_1024, 'mask_BxS_ff1': mask_BxS_ff1, 'mask_BxS2_ik0': mask_BxS2_ik0, 'L0_attn_Wq': _L0_attn_in['Wq'], 'L0_attn_Wk': _L0_attn_in['Wk'], 'L0_attn_Wv': _L0_attn_in['Wv'], 'L0_attn_Wo': _L0_attn_in['Wo'], 'L0_attn_bo': _L0_attn_in['bo'], 'L0_attn_gamma': _L0_attn_in['gamma'], 'L0_attn_beta': _L0_attn_in['beta'], 'L0_xattn_Ws': _L0_xattn_in['Ws'], 'L0_xattn_W': _L0_xattn_in['W'], 'L0_xattn_w': _L0_xattn_in['w'], 'L0_xattn_b': _L0_xattn_in['b'], 'L0_xattn_Wcw': _L0_xattn_in['Wcw'], 'L0_xattn_bcw': _L0_xattn_in['bcw'], 'L0_xattn_Wcb': _L0_xattn_in['Wcb'], 'L0_xattn_bcb': _L0_xattn_in['bcb'], 'L0_ffn_gate_w': _L0_ffn_in['gate_w'], 'L0_ffn_gate_b': _L0_ffn_in['gate_b'], 'L0_ffn_w1': _L0_ffn_in['w1'], 'L0_ffn_b1': _L0_ffn_in['b1'], 'L0_ffn_w2': _L0_ffn_in['w2'], 'L0_ffn_b2': _L0_ffn_in['b2'], 'L0_ffn_wg': _L0_ffn_in['wg'], 'L0_ffn_bg': _L0_ffn_in['bg'], 'L0_ffn_w3': _L0_ffn_in['w3'], 'L0_ffn_b3': _L0_ffn_in['b3']}

def reference(x, ctx_1024, mask_BxS_ff1, mask_BxS2_ik0, L0_attn_Wq, L0_attn_Wk, L0_attn_Wv, L0_attn_Wo, L0_attn_bo, L0_attn_gamma, L0_attn_beta, L0_xattn_Ws, L0_xattn_W, L0_xattn_w, L0_xattn_b, L0_xattn_Wcw, L0_xattn_bcw, L0_xattn_Wcb, L0_xattn_bcb, L0_ffn_gate_w, L0_ffn_gate_b, L0_ffn_w1, L0_ffn_b1, L0_ffn_w2, L0_ffn_b2, L0_ffn_wg, L0_ffn_bg, L0_ffn_w3, L0_ffn_b3):
    import jax
    import jax.numpy as jnp

    def _L0_attn_ref(x, Wq, Wk, Wv, Wo, bo, gamma, beta):
        import jax, jax.numpy as jnp
        import numpy as np
        B, L, D = (8, 512, 128)
        LN_EPS = 1e-05

        def _linear_attn(q, k, v):
            d = q.shape[-1]
            q = jax.nn.softmax(q, axis=-1) * d ** (-0.5)
            k = jax.nn.softmax(k, axis=-2)
            context = jnp.einsum('bld,ble->bde', k, v)
            return jnp.einsum('bld,bde->ble', q, context)

        def _layernorm(x, gamma, beta):
            mu = jnp.mean(x, axis=-1, keepdims=True)
            var = jnp.var(x, axis=-1, keepdims=True)
            return (x - mu) * jax.lax.rsqrt(var + LN_EPS) * gamma + beta
        q = jnp.einsum('bld,de->ble', x, Wq)
        k = jnp.einsum('bld,de->ble', x, Wk)
        v = jnp.einsum('bld,de->ble', x, Wv)
        attn = _linear_attn(q, k, v)
        out = jnp.einsum('ble,ed->bld', attn, Wo) + bo
        return _layernorm(x + out, gamma, beta)

    def _L0_xattn_ref(features, masks, textual_features, q_masks, Ws, W, w, b, Wcw, bcw, Wcb, bcb):
        import jax, jax.numpy as jnp
        import numpy as np
        B, F, T, D = (8, 32, 32, 128)
        NEG = -1e+30
        txt_proj = jnp.einsum('btd,de->bte', textual_features, Ws)
        feat_proj = jnp.einsum('bfd,de->bfe', features, W)
        h = jnp.tanh(txt_proj[:, None, :, :] + feat_proj[:, :, None, :] + b[None, None, :, :][..., 0, :])
        rho = jnp.einsum('bftd,d->bft', h, w[:, 0])
        qm = q_masks.astype(jnp.float32)
        rho = rho + (1.0 - qm)[:, None, :] * NEG
        att = jax.nn.softmax(rho, axis=-1)
        txt_h = jnp.einsum('bft,btd->bfd', att, textual_features)
        w_s = jnp.tanh(jnp.einsum('bfd,od->bfo', txt_h, Wcw) + bcw)
        b_s = jnp.tanh(jnp.einsum('bfd,od->bfo', txt_h, Wcb) + bcb)
        return w_s * features + b_s

    def _L0_ffn_ref(x, gate_w, gate_b, w1, b1, w2, b2, wg, bg, w3, b3):
        import jax, jax.numpy as jnp
        import numpy as np
        B, S, H = (2, 128, 128)
        DFF = 256
        E = 8
        TOPK = 2

        def _expert_ffn(x, w1, b1, w2, b2, wg, bg, w3, b3):
            x1 = jnp.einsum('bsh,hf->bsf', x, w1) + b1
            x2 = jnp.einsum('bsh,hf->bsf', x, w2) + b2
            z = x1 * x2
            s = jax.nn.silu(jnp.einsum('bsf,fg->bsg', z, wg) + bg)
            return jnp.einsum('bsg,gh->bsh', s, w3) + b3
        logits = jnp.einsum('bsh,he->bse', x, gate_w) + gate_b
        topv, topi = jax.lax.top_k(logits, TOPK)
        probs = jax.nn.softmax(topv, axis=-1)
        out = jnp.zeros_like(x)
        for e in range(E):
            we = jnp.sum(probs * (topi == e), axis=-1)
            y = _expert_ffn(x, w1[e], b1[e], w2[e], b2[e], wg[e], bg[e], w3[e], b3[e])
            out = out + we[..., None] * y
        return out
    x = x + _L0_attn_ref(_layernorm(x, axis=-1), L0_attn_Wq, L0_attn_Wk, L0_attn_Wv, L0_attn_Wo, L0_attn_bo, L0_attn_gamma, L0_attn_beta)
    x = x + _L0_xattn_ref(_layernorm(x, axis=-1), mask_BxS_ff1, ctx_1024, mask_BxS2_ik0, L0_xattn_Ws, L0_xattn_W, L0_xattn_w, L0_xattn_b, L0_xattn_Wcw, L0_xattn_bcw, L0_xattn_Wcb, L0_xattn_bcb)
    x = x + _L0_ffn_ref(_layernorm(x, axis=-1), L0_ffn_gate_w, L0_ffn_gate_b, L0_ffn_w1, L0_ffn_b1, L0_ffn_w2, L0_ffn_b2, L0_ffn_wg, L0_ffn_bg, L0_ffn_w3, L0_ffn_b3)
    return x

_drawn_inputs = setup_inputs


def setup_inputs(seed=0):
    import zlib

    import numpy as np

    out = dict(_drawn_inputs(seed))
    spreads = {'L0_attn_bo': (0.0, 0.1),
     'L0_attn_gamma': (1.0, 0.2),
     'L0_attn_beta': (0.0, 0.1),
     'L0_ffn_gate_b': (0.0, 0.363),
     'L0_ffn_b1': (0.0, 0.8),
     'L0_ffn_b2': (0.0, 0.8),
     'L0_ffn_bg': (0.0, 0.8),
     'L0_ffn_b3': (0.0, 0.8)}
    factors = {'L0_attn_Wq': 8.0,
     'L0_attn_Wk': 8.0,
     'L0_attn_Wv': 8.0,
     'L0_attn_Wo': 8.0,
     'L0_xattn_W': 25.368,
     'L0_xattn_b': 64.0,
     'L0_ffn_w1': 8.0,
     'L0_ffn_w2': 8.0,
     'L0_ffn_wg': 8.0,
     'L0_ffn_w3': 8.0,
     'L0_xattn_Ws': 8.0,
     'L0_xattn_w': 8.0,
     'L0_xattn_Wcw': 3.283}
    for name, (base, spread) in spreads.items():
        noise = np.random.default_rng([zlib.crc32(name.encode()), seed]).standard_normal(out[name].shape)
        drawn = base * np.exp(spread * noise) if base else spread * noise
        out[name] = jnp.asarray(drawn.astype(out[name].dtype))
    for name, factor in factors.items():
        out[name] = (out[name] * factor).astype(out[name].dtype)
    return out
```

```python
from contextlib import ExitStack

import concourse.bass as bass
from concourse import mybir

ALU = mybir.AluOpType
ACT = mybir.ActivationFunctionType
F32 = mybir.dt.float32
I32 = mybir.dt.int32
U32 = mybir.dt.uint32
X = mybir.AxisListType.X

P = 128
EPS = 1e-5
NEG = -1e30
RING = 3
GROUP = 6
PER_STEP = 3
EXPERTS_PER_STEP = 2


def decoder_layer_program(nc, x, ctx, q_mask, Wq, Wk, Wv, Wo, bo, gamma, beta, Ws, W, w, xb, Wcw, bcw,
                          Wcb, bcb, gate_w, gate_b, w1, b1, w2, b2, wg, bg, w3, b3, out):
    B, L, D = x.shape
    T = ctx.shape[1]
    E, _, FF = w1.shape
    C = L // P
    FC = FF // P
    STEPS = E // EXPERTS_PER_STEP
    FIRST = T - STEPS * PER_STEP * GROUP
    GROUPS = 1 + STEPS * PER_STEP
    assert D == P and L == C * P and 0 < FIRST <= GROUP
    LN = {}
    for kind in [("in", b) for b in range(B)] + [(k, b) for b in range(B) for k in ("attn", "x")] + \
            [("ffn", b) for b in range(B)]:
        LN[kind] = len(LN)
    XB, WX, WCW, WCB = 3 * E * FC, 3 * E * FC + 1, 3 * E * FC + 2, 3 * E * FC + 3
    NROWS = 3 * E * FC + 4

    with ExitStack() as stack:
        def sb(name, shape, dt=F32):
            return stack.enter_context(nc.sbuf_tensor(name, shape, dt))

        def sem(name):
            return stack.enter_context(nc.semaphore(name))

        bank = [stack.enter_context(nc.psum_tensor(f"bank{i}", [P, 512], F32)) for i in range(8)]

        x_sb = sb("x_sb", [P, B * C, D])
        ctx_sb = sb("ctx_sb", [T, B, D])
        mask_i = sb("mask_i", [P, B, T], I32)
        wqkvo = sb("wqkvo", [P, 4, D])
        xw = sb("xw", [P, 2, D])
        rows = sb("rows", [NROWS, P])
        ln_rows = sb("ln_rows", [P, 3, D])
        small = sb("small", [P, E + 2])
        gate_sb = sb("gate_sb", [P, E])
        b3_sb = sb("b3_sb", [E, D])
        w1_sb = sb("w1_sb", [P, 2, FF])
        w2_sb = sb("w2_sb", [P, 2, FF])
        wg_sb = sb("wg_sb", [P, 2, FC, FF])
        w3_sb = sb("w3_sb", [P, 2, FC, D])
        ident = sb("ident", [P, P])
        expert_i = sb("expert_i", [P, E], I32)
        expert_id = sb("expert_id", [P, E])
        minus_half = sb("minus_half", [P, C])
        cols = sb("cols", [P, NROWS])
        ctxT = sb("ctxT", [P, B * T])
        WvT = sb("WvT", [P, P])
        WvWo = sb("WvWo", [P, P])
        txtT = sb("txtT", [P, B * T])
        cwcb = sb("cwcb", [P, 2, B * T])
        mask_f = sb("mask_f", [P, B, T])
        stats = sb("stats", [P, C, 6])
        moments = sb("moments", [P, C, 2])
        var_eps = sb("var_eps", [P, C])
        rstd = sb("rstd", [P, C])
        h0 = sb("h0", [P, B, C, D])
        h0bo = sb("h0bo", [P, B, C, D])
        xbeta = sb("xbeta", [P, B, C, D])
        h0T = sb("h0T", [P, B, L])
        neg_qmax = sb("neg_qmax", [P, B, C])
        qsum = sb("qsum", [P, B, C])
        rq = sb("rq", [P, B, C])
        qE = sb("qE", [P, B, C, D])
        qET = sb("qET", [P, B, L])
        neg_kmax = sb("neg_kmax", [P, B])
        ksum = sb("ksum", [P, B])
        rk = sb("rk", [P, B])
        kET = sb("kET", [P, B, L])
        kE = sb("kE", [P, B, C, D])
        AT = sb("AT", [P, B, P])
        Cm = sb("Cm", [P, B, P])
        res = sb("res", [P, B, C, D])
        nrm = sb("nrm", [P, B, C, D])
        x1 = sb("x1", [P, B, C, D])
        h1 = sb("h1", [P, B, C, D])
        h1T = sb("h1T", [P, B, L])
        FT = sb("FT", [P, B, L])
        pre = sb("pre", [P, RING, GROUP, L])
        tanh_out = sb("tanh_out", [P, RING, GROUP, L])
        rho = sb("rho", [P, C, T])
        rmax = sb("rmax", [P, C])
        att = sb("att", [P, 3, C, T])
        sums = sb("sums", [P, 3, C])
        rden = sb("rden", [P, C])
        wsbs_pre = sb("wsbs_pre", [P, 2, C])
        wsbs = sb("wsbs", [P, 2, C])
        x2 = sb("x2", [P, C, D])
        h2 = sb("h2", [P, C, D])
        h2T = sb("h2T", [P, B, L])
        logits = sb("logits", [P, C, E])
        top = sb("top", [P, C, 8])
        top_i = sb("top_i", [P, C, 8], U32)
        top_f = sb("top_f", [P, C, 8])
        dtop = sb("dtop", [P, C])
        etop = sb("etop", [P, C])
        p1 = sb("p1", [P, C])
        p2 = sb("p2", [P, C])
        we1 = sb("we1", [P, C, E])
        we = sb("we", [P, B, C, E])
        weT = sb("weT", [E, L])
        x2b = sb("x2b", [P, FC, L])
        z = sb("z", [P, FC, L])
        s = sb("s", [P, FC, L])
        acc = sb("acc", [P, B, C, D])

        x_in = [sem(f"x_in{b}") for b in range(B)]
        attn_w_in, ctx_in, rows_in, ln_rows_in, xw_in, small_in = (
            sem(n) for n in ("attn_w_in", "ctx_in", "rows_in", "ln_rows_in", "xw_in", "small_in"))
        expert_w_in = [sem(f"expert_w_in{h}") for h in range(EXPERTS_PER_STEP)]
        out_stored = sem("out_stored")
        zeroed, ident_ready, consts_ready, rstd_ready, pool_rows = (
            sem(n) for n in ("zeroed", "ident_ready", "consts_ready", "rstd_ready", "pool_rows"))
        chain = sem("vector_chain")
        var_ready = sem("var_ready")
        v = {n: sem("v_" + n) for n in (
            "cols", "WvT", "WvWo", "txt", "h0", "neg_kmax", "neg_qmax", "kE", "AT", "C", "h1", "added",
            "exp_in", "wsbs_pre", "h2", "dtop", "we", "weT", "z", "acc", "rho_read")}
        a = {n: sem("a_" + n) for n in (
            "h0T", "kexp", "qexp", "qET", "h1T", "FT", "tanh", "att", "wsbs", "h2T", "etop", "x2b", "silu")}
        t = {n: sem("t_" + n) for n in (
            "cols", "WvWo", "txt", "h0T", "q", "k", "kE", "qET", "AT", "C", "out", "h1T", "FT", "rho",
            "h2T", "gate", "weT", "b3", "x12", "g", "y")}

        block = stack.enter_context(nc.Block())

        def text_group(b, step, j):
            if step is None:
                return b * T, FIRST, 0, GROUPS * b
            return b * T + FIRST + (step * PER_STEP + j) * GROUP, GROUP, (1 + j) % RING, \
                GROUPS * b + 1 + step * PER_STEP + j

        def expert_no(b, step, j):
            return E * b + step * EXPERTS_PER_STEP + j

        @block.sync
        def _(sp):
            for b in range(B):
                sp.dma_start(x_sb[:, b * C:(b + 1) * C, :],
                             x[b].rearrange("(c p) d -> p c d", p=P)).then_inc(x_in[b], 16)
            for i, m in enumerate((Wq, Wk, Wv, Wo)):
                sp.dma_start(wqkvo[:, i, :], m).then_inc(attn_w_in, 16)
            for i, m in enumerate((bo, gamma, beta)):
                sp.dma_start(ln_rows[:, i, :], m.rearrange("(o d) -> o d", o=1).broadcast_to([P, D]))\
                    .then_inc(ln_rows_in, 16)
            for i, m in enumerate((Ws, W)):
                sp.dma_start(xw[:, i, :], m).then_inc(xw_in, 16)

            def load_expert(e, h):
                sp.dma_start(w1_sb[:, h, :], w1[e]).then_inc(expert_w_in[h], 16)
                sp.dma_start(w2_sb[:, h, :], w2[e]).then_inc(expert_w_in[h], 16)
                sp.dma_start(wg_sb[:, h, :, :], wg[e].rearrange("(k p) f -> p k f", p=P))\
                    .then_inc(expert_w_in[h], 16)
                sp.dma_start(w3_sb[:, h, :, :], w3[e].rearrange("(k p) f -> p k f", p=P))\
                    .then_inc(expert_w_in[h], 16)

            for h in range(EXPERTS_PER_STEP):
                load_expert(h, h)
            for b in range(B):
                with sp.Fori(1 if b == 0 else 0, STEPS) as step:
                    for h in range(EXPERTS_PER_STEP):
                        sp.wait_ge(t["y"], expert_no(b, step, h) - 1)
                        load_expert(step * EXPERTS_PER_STEP + h, h)
                sp.wait_ge(v["acc"], E * (b + 1))
                sp.dma_start(out[b].rearrange("(c p) d -> p c d", p=P), acc[:, b, :, :])\
                    .then_inc(out_stored, 16)
            sp.wait_ge(out_stored, 16 * B)

        @block.gpsimd
        def _(pool):
            nc.gpsimd.memset(ident[:], 0.0).then_inc(zeroed, 1)
            nc.gpsimd.memset(minus_half[:], -0.5).then_inc(consts_ready, 1)
            nc.gpsimd.iota(expert_i[:], pattern=[[1, E]], base=0, channel_multiplier=0)\
                .then_inc(consts_ready, 1)
            pool.wait_ge(zeroed, 1)
            nc.gpsimd.affine_select(out=ident[:], in_=ident[:], compare_op=ALU.not_equal, fill=1.0, base=0,
                                    pattern=[[-1, P]], channel_multiplier=1).then_inc(ident_ready, 1)
            pool.wait_ge(consts_ready, 2)

            def rstd_of():
                nonlocal ln
                pool.wait_ge(var_ready, ln + 1)
                nc.gpsimd.tensor_tensor(rstd[:], var_eps[:], minus_half[:], ALU.pow)\
                    .then_inc(rstd_ready, 1)
                ln += 1

            ln = 0
            for b in range(B):
                rstd_of()
            pool.wait_ge(ln_rows_in, 16 * 3)
            for b in range(B):
                pool.wait_ge(v["h0"], b + 1)
                nc.gpsimd.tensor_tensor(h0bo[:, b], h0[:, b],
                                        ln_rows[:, 0:1, :].broadcast_to([P, C, D]), ALU.add)\
                    .then_inc(pool_rows, 1)
                nc.gpsimd.tensor_tensor(xbeta[:, b], x_sb[:, b * C:(b + 1) * C, :],
                                        ln_rows[:, 2:3, :].broadcast_to([P, C, D]), ALU.add)\
                    .then_inc(pool_rows, 1)
            for b in range(B):
                rstd_of()
                rstd_of()
            for b in range(B):
                rstd_of()

        @block.scalar
        def _(act):
            act.dma_start(rows[0:E * FC, :], b1.rearrange("e (c p) -> (e c) p", p=P)).then_inc(rows_in, 16)
            act.dma_start(rows[E * FC:2 * E * FC, :], b2.rearrange("e (c p) -> (e c) p", p=P))\
                .then_inc(rows_in, 16)
            act.dma_start(rows[2 * E * FC:3 * E * FC, :], bg.rearrange("e (c p) -> (e c) p", p=P))\
                .then_inc(rows_in, 16)
            act.dma_start(rows[XB:XB + 1, :], xb).then_inc(rows_in, 16)
            act.dma_start(rows[WX:WX + 1, :], w.rearrange("d o -> o d")).then_inc(rows_in, 16)
            act.dma_start(rows[WCW:WCW + 1, :], Wcw).then_inc(rows_in, 16)
            act.dma_start(rows[WCB:WCB + 1, :], Wcb).then_inc(rows_in, 16)
            act.dma_start(ctx_sb[:], ctx.rearrange("b t d -> t b d")).then_inc(ctx_in, 16)
            act.dma_start(mask_i[:], q_mask.rearrange("(o b) t -> o b t", o=1).broadcast_to([P, B, T]))\
                .then_inc(small_in, 16)
            act.dma_start(small[:, 0:E], gate_b.rearrange("(o e) -> o e", o=1).broadcast_to([P, E]))\
                .then_inc(small_in, 16)
            act.dma_start(small[:, E:E + 1], bcw.rearrange("(o e) -> o e", o=1).broadcast_to([P, 1]))\
                .then_inc(small_in, 16)
            act.dma_start(small[:, E + 1:E + 2], bcb.rearrange("(o e) -> o e", o=1).broadcast_to([P, 1]))\
                .then_inc(small_in, 16)
            act.dma_start(gate_sb[:], gate_w).then_inc(small_in, 16)
            act.dma_start(b3_sb[:], b3).then_inc(small_in, 16)

            def attention(b):
                A, Q, K, M = bank[4 * b:4 * b + 4]
                act.wait_ge(t["h0T"], b + 1)
                nc.scalar.copy(h0T[:, b, :], A[:, :]).then_inc(a["h0T"], 1)
                act.wait_ge(t["k"], b + 1)
                act.wait_ge(v["neg_kmax"], b + 1)
                nc.scalar.activation(kET[:, b, :], K[:, :], ACT.Exp, bias=neg_kmax[:, b:b + 1],
                                     accum_out=ksum[:, b:b + 1]).then_inc(a["kexp"], 1)
                act.wait_ge(v["neg_qmax"], b + 1)
                for c in range(C):
                    nc.scalar.activation(qE[:, b, c, :], Q[:, c * P:(c + 1) * P], ACT.Exp,
                                         bias=neg_qmax[:, b, c:c + 1],
                                         accum_out=qsum[:, b, c:c + 1]).then_inc(a["qexp"], 1)
                act.wait_ge(t["qET"], b + 1)
                nc.scalar.copy(qET[:, b, :], Q[:, :]).then_inc(a["qET"], 1)

            def features(b):
                A, M = bank[4 * b], bank[4 * b + 3]
                act.wait_ge(t["h1T"], b + 1)
                nc.scalar.copy(h1T[:, b, :], M[:, :]).then_inc(a["h1T"], 1)
                act.wait_ge(t["FT"], b + 1)
                nc.scalar.activation(FT[:, b, :], A[:, :], ACT.Identity, bias=cols[:, XB:XB + 1])\
                    .then_inc(a["FT"], 1)

            def tanh_group(b, step, j):
                _, n, slot, g = text_group(b, step, j)
                act.wait_ge(v["added"], g + 1)
                used = g if step is None else g - RING + 1
                if not (isinstance(used, int) and used <= 0):
                    act.wait_ge(t["rho"], used)
                nc.scalar.activation(tanh_out[:, slot, 0:n, :], pre[:, slot, 0:n, :], ACT.Tanh)\
                    .then_inc(a["tanh"], 1)

            def cross_end(b):
                act.wait_ge(v["exp_in"], b + 1)
                nc.scalar.activation(att[:, 0, :, :], rho[:], ACT.Exp).then_inc(a["att"], 1)
                act.wait_ge(v["wsbs_pre"], b + 1)
                nc.scalar.activation(wsbs[:, 0, :], wsbs_pre[:, 0, :], ACT.Tanh, bias=small[:, E:E + 1])
                nc.scalar.activation(wsbs[:, 1, :], wsbs_pre[:, 1, :], ACT.Tanh,
                                     bias=small[:, E + 1:E + 2]).then_inc(a["wsbs"], 1)
                act.wait_ge(t["h2T"], b + 1)
                nc.scalar.copy(h2T[:, b, :], bank[7][:, :]).then_inc(a["h2T"], 1)
                act.wait_ge(v["dtop"], b + 1)
                nc.scalar.activation(etop[:], dtop[:], ACT.Exp).then_inc(a["etop"], 1)

            def gate_half(b, step, h):
                n = expert_no(b, step, h)
                for c in range(FC):
                    act.wait_ge(t["x12"], FC * n + c + 1)
                    if not (b == 0 and h == 0):
                        act.wait_ge(v["z"], FC * n - FC + c + 1)
                    elif b == 0:
                        act.wait_ge(v["z"], FC * n)
                    e = step * EXPERTS_PER_STEP + h
                    nc.scalar.activation(x2b[:, c, :], bank[2 * c + 1][:, :], ACT.Identity,
                                         bias=cols[:, bass.ds(E * FC + FC * e + c, 1)]).then_inc(a["x2b"], 1)

            def silu_half(b, step, h):
                n = expert_no(b, step, h)
                e = step * EXPERTS_PER_STEP + h
                for c in range(FC):
                    act.wait_ge(t["g"], FC * n + c + 1)
                    nc.scalar.activation(s[:, c, :], bank[4 + c][:, :], ACT.Silu,
                                         bias=cols[:, bass.ds(2 * E * FC + FC * e + c, 1)])\
                        .then_inc(a["silu"], 1)

            act.wait_ge(v["cols"], 1)
            act.wait_ge(small_in, 16 * 6)
            for b in range(B):
                attention(b)
                features(b)
            tanh_group(0, None, 0)
            for j in range(PER_STEP):
                tanh_group(0, 0, j)
            with act.Fori(1, STEPS) as step:
                for j in range(PER_STEP):
                    tanh_group(0, step, j)
            cross_end(0)
            for b in range(B):
                if b + 1 < B:
                    tanh_group(b + 1, None, 0)
                with act.Fori(0, STEPS) as step:
                    for h in range(EXPERTS_PER_STEP):
                        gate_half(b, step, h)
                        if b + 1 < B:
                            tanh_group(b + 1, step, h)
                        silu_half(b, step, h)
                    if b + 1 < B:
                        for j in range(EXPERTS_PER_STEP, PER_STEP):
                            tanh_group(b + 1, step, j)
                if b + 1 < B:
                    cross_end(b + 1)

        @block.tensor
        def _(pe):
            def transposed(out_ap, in_ap, k):
                return nc.tensor.transpose(out_ap, in_ap, ident[0:k, 0:k])

            def attention(b):
                A, Q, K, M = bank[4 * b:4 * b + 4]
                pe.wait_ge(v["h0"], b + 1)
                for c in range(C):
                    mm = transposed(A[:, c * P:(c + 1) * P], h0[:, b, c, :], P)
                mm.then_inc(t["h0T"], 1)
                pe.wait_ge(a["h0T"], b + 1)
                pe.wait_ge(attn_w_in, 64)
                nc.tensor.matmul(K[:, :], wqkvo[:, 1, :], h0T[:, b, :], start=True, stop=True)\
                    .then_inc(t["k"], 1)
                for c in range(C):
                    mm = nc.tensor.matmul(Q[:, c * P:(c + 1) * P], h0T[:, b, c * P:(c + 1) * P],
                                          wqkvo[:, 0, :], start=True, stop=True)
                mm.then_inc(t["q"], 1)
                pe.wait_ge(a["kexp"], b + 1)
                for c in range(C):
                    mm = transposed(A[:, c * P:(c + 1) * P], kET[:, b, c * P:(c + 1) * P], P)
                mm.then_inc(t["kE"], 1)
                pe.wait_ge(a["qexp"], C * (b + 1))
                for c in range(C):
                    mm = transposed(Q[:, c * P:(c + 1) * P], qE[:, b, c, :], P)
                mm.then_inc(t["qET"], 1)
                pe.wait_ge(v["kE"], b + 1)
                for c in range(C):
                    mm = nc.tensor.matmul(K[:, 0:P], h0[:, b, c, :], kE[:, b, c, :],
                                          start=(c == 0), stop=(c == C - 1))
                mm.then_inc(t["AT"], 1)
                pe.wait_ge(v["AT"], b + 1)
                nc.tensor.matmul(K[:, P:2 * P], AT[:, b, :], WvWo[:], start=True, stop=True)\
                    .then_inc(t["C"], 1)
                pe.wait_ge(a["qET"], b + 1)
                pe.wait_ge(v["C"], b + 1)
                for c in range(C):
                    mm = nc.tensor.matmul(A[:, c * P:(c + 1) * P], qET[:, b, c * P:(c + 1) * P],
                                          Cm[:, b, :], start=True, stop=True)
                mm.then_inc(t["out"], 1)

            def features(b):
                A, M = bank[4 * b], bank[4 * b + 3]
                pe.wait_ge(v["h1"], b + 1)
                for c in range(C):
                    mm = transposed(M[:, c * P:(c + 1) * P], h1[:, b, c, :], P)
                mm.then_inc(t["h1T"], 1)
                pe.wait_ge(a["h1T"], b + 1)
                nc.tensor.matmul(A[:, :], xw[:, 1, :], h1T[:, b, :], start=True, stop=True)\
                    .then_inc(t["FT"], 1)

            def score_group(b, step, j):
                t0, n, slot, g = text_group(b, step, j)
                pe.wait_ge(a["tanh"], g + 1)
                for i in range(n):
                    for c in range(C):
                        mm = nc.tensor.matmul(bank[7][:, bass.ds(t0 - b * T + i + c * T, 1)],
                                              tanh_out[:, slot, i, c * P:(c + 1) * P],
                                              cols[:, WX:WX + 1], start=True, stop=True)
                mm.then_inc(t["rho"], 1)

            def cross_end(b):
                R = bank[7]
                pe.wait_ge(v["h2"], b + 1)
                for c in range(C):
                    mm = transposed(R[:, c * P:(c + 1) * P], h2[:, c, :], P)
                mm.then_inc(t["h2T"], 1)
                pe.wait_ge(a["h2T"], b + 1)
                for c in range(C):
                    mm = nc.tensor.matmul(R[:, c * E:(c + 1) * E], h2T[:, b, c * P:(c + 1) * P],
                                          gate_sb[:], start=True, stop=True)
                mm.then_inc(t["gate"], 1)
                pe.wait_ge(v["we"], b + 1)
                for c in range(C):
                    mm = transposed(R[0:E, c * P:(c + 1) * P], we[:, b, c, :], P)
                mm.then_inc(t["weT"], 1)
                pe.wait_ge(v["weT"], b + 1)
                for c in range(C):
                    mm = nc.tensor.matmul(R[:, c * P:(c + 1) * P], weT[:, c * P:(c + 1) * P],
                                          b3_sb[:], start=True, stop=True)
                mm.then_inc(t["b3"], 1)

            def expert_up(b, step, h):
                n = expert_no(b, step, h)
                pe.wait_ge(expert_w_in[h], (step + (STEPS * b + 1)) * 64)
                for c in range(FC):
                    if not (b == 0 and h == 0):
                        pe.wait_ge(v["z"], FC * n - FC + c + 1)
                    else:
                        pe.wait_ge(v["z"], FC * n)
                    nc.tensor.matmul(bank[2 * c][:, :], w1_sb[:, h, c * P:(c + 1) * P], h2T[:, b, :],
                                     start=True, stop=True)
                    nc.tensor.matmul(bank[2 * c + 1][:, :], w2_sb[:, h, c * P:(c + 1) * P], h2T[:, b, :],
                                     start=True, stop=True).then_inc(t["x12"], 1)

            def expert_gate(b, step, h):
                n = expert_no(b, step, h)
                for c in range(FC):
                    if not (b == 0 and h == 0):
                        pe.wait_ge(a["silu"], FC * n - FC + c + 1)
                    else:
                        pe.wait_ge(a["silu"], FC * n)
                    for k in range(FC):
                        if c == 0:
                            pe.wait_ge(v["z"], FC * n + k + 1)
                        mm = nc.tensor.matmul(bank[4 + c][:, :], wg_sb[:, h, k, c * P:(c + 1) * P],
                                              z[:, k, :], start=(k == 0), stop=(k == FC - 1))
                    mm.then_inc(t["g"], 1)

            def expert_down(b, step, h):
                n = expert_no(b, step, h)
                pe.wait_ge(a["silu"], FC * n + FC)
                pe.wait_ge(v["acc"], n)
                for c in range(C):
                    for k in range(FC):
                        mm = nc.tensor.matmul(bank[6][:, c * P:(c + 1) * P], s[:, k, c * P:(c + 1) * P],
                                              w3_sb[:, h, k, :], start=(k == 0), stop=(k == FC - 1))
                mm.then_inc(t["y"], 1)

            pe.wait_ge(ident_ready, 1)
            pe.wait_ge(rows_in, 16 * 7)
            transposed(bank[7][:, 0:NROWS], rows[:], NROWS)
            pe.wait_ge(ctx_in, 16)
            for b in range(B):
                transposed(bank[7][:, NROWS + b * T:NROWS + (b + 1) * T], ctx_sb[:, b, :], T)
            pe.wait_ge(attn_w_in, 64)
            transposed(bank[7][:, 256:384], wqkvo[:, 2, :], P).then_inc(t["cols"], 1)
            pe.wait_ge(v["cols"], 1)
            nc.tensor.matmul(bank[6][:, 0:P], WvT[:], wqkvo[:, 3, :], start=True, stop=True)\
                .then_inc(t["WvWo"], 1)
            pe.wait_ge(xw_in, 32)
            nc.tensor.matmul(bank[7][:, 0:B * T], xw[:, 0, :], ctxT[:], start=True, stop=True)
            for i, col in enumerate((WCW, WCB)):
                mm = nc.tensor.matmul(bank[7][:, (1 + i) * B * T:(2 + i) * B * T],
                                      cols[:, col:col + 1].broadcast_to([P, P]), ctxT[:],
                                      start=True, stop=True)
            mm.then_inc(t["txt"], 1)
            attention(0)
            pe.wait_ge(v["WvWo"], 1)
            pe.wait_ge(v["txt"], 1)
            features(0)
            for b in range(1, B):
                attention(b)
                features(b)
            score_group(0, None, 0)
            with pe.Fori(0, STEPS) as step:
                for j in range(PER_STEP):
                    score_group(0, step, j)
            cross_end(0)
            for b in range(B):
                more = b + 1 < B
                if more:
                    pe.wait_ge(v["rho_read"], 2 * b + 2)
                    score_group(b + 1, None, 0)
                with pe.Fori(0, STEPS) as step:
                    expert_up(b, step, 0)
                    if more:
                        score_group(b + 1, step, 0)
                    expert_gate(b, step, 0)
                    expert_up(b, step, 1)
                    if more:
                        score_group(b + 1, step, 1)
                    expert_down(b, step, 0)
                    expert_gate(b, step, 1)
                    if more:
                        score_group(b + 1, step, 2)
                    expert_down(b, step, 1)
                if more:
                    cross_end(b + 1)

        @block.vector
        def _(dve):
            links = 0

            def link(ins):
                nonlocal links
                links += 1
                ins.then_inc(chain, 1)
                dve.wait_ge(chain, links)

            def layer_norm(which, src, dst, done=None, n=1):
                for c in range(C):
                    last = nc.vector.bn_stats(stats[:, c, :], src[:, c, :])
                link(last)
                for c in range(C):
                    last = nc.vector.bn_aggr(moments[:, c, :], stats[:, c, :])
                link(last)
                nc.vector.tensor_scalar(var_eps[:], moments[:, :, 1], EPS, None, ALU.add)\
                    .then_inc(var_ready, 1)
                dve.wait_ge(rstd_ready, LN[which] + 1)
                for c in range(C):
                    last = nc.vector.tensor_scalar(dst[:, c, :], src[:, c, :], moments[:, c, 0:1],
                                                   rstd[:, c:c + 1], ALU.subtract, ALU.mult)
                if done is None:
                    link(last)
                else:
                    last.then_inc(done, 1)

            def attention(b):
                A, Q, K, M = bank[4 * b:4 * b + 4]
                dve.wait_ge(t["k"], b + 1)
                nc.vector.tensor_reduce(neg_kmax[:, b:b + 1], K[:, :], X, ALU.max, negate=True)\
                    .then_inc(v["neg_kmax"], 1)
                dve.wait_ge(t["q"], b + 1)
                nc.vector.tensor_reduce(neg_qmax[:, b, :], Q[:, :].rearrange("p (c d) -> p c d", c=C), X,
                                        ALU.max, negate=True).then_inc(v["neg_qmax"], 1)
                dve.wait_ge(t["kE"], b + 1)
                nc.vector.tensor_copy(kE[:, b].rearrange("p c d -> p (c d)"), A[:, :]).then_inc(v["kE"], 1)
                dve.wait_ge(a["kexp"], b + 1)
                link(nc.vector.reciprocal(rk[:, b:b + 1], ksum[:, b:b + 1]))
                dve.wait_ge(a["qexp"], C * (b + 1))
                nc.vector.reciprocal(rq[:, b, :], qsum[:, b, :])
                dve.wait_ge(t["AT"], b + 1)
                nc.vector.tensor_copy(AT[:, b, :], K[:, 0:P]).then_inc(v["AT"], 1)
                dve.wait_ge(t["C"], b + 1)
                nc.vector.tensor_scalar(Cm[:, b, :], K[:, P:2 * P], rk[:, b:b + 1], float(D) ** -0.5,
                                        ALU.mult, ALU.mult).then_inc(v["C"], 1)
                dve.wait_ge(t["out"], b + 1)
                dve.wait_ge(pool_rows, 2 * (b + 1))
                dve.wait_ge(v["C"], b + 1)
                for c in range(C):
                    last = nc.vector.scalar_tensor_tensor(out=res[:, b, c, :], in0=A[:, c * P:(c + 1) * P],
                                                          scalar=rq[:, b, c:c + 1], in1=h0bo[:, b, c, :],
                                                          op0=ALU.mult, op1=ALU.add)
                link(last)
                layer_norm(("attn", b), res[:, b], nrm[:, b])
                link(nc.vector.tensor_tensor(nrm[:, b], nrm[:, b],
                                             ln_rows[:, 1:2, :].broadcast_to([P, C, D]), ALU.mult))
                link(nc.vector.tensor_tensor(x1[:, b], nrm[:, b], xbeta[:, b], ALU.add))
                layer_norm(("x", b), x1[:, b], h1[:, b], v["h1"])

            def add_group(b, step, j):
                t0, n, slot, g = text_group(b, step, j)
                used = g if step is None else g - RING + 1
                if not (isinstance(used, int) and used <= 0):
                    dve.wait_ge(a["tanh"], used)
                for i in range(n):
                    last = nc.vector.tensor_scalar(pre[:, slot, i, :], FT[:, b, :],
                                                   txtT[:, bass.ds(t0 + i, 1)], None, ALU.add)
                last.then_inc(v["added"], 1)

            def cross_end(b):
                R = bank[7]
                dve.wait_ge(t["rho"], GROUPS * (b + 1))
                if b > 0:
                    dve.wait_ge(a["att"], b)
                link(nc.vector.tensor_tensor(rho[:], R[:, 0:C * T].rearrange("p (c t) -> p c t", c=C),
                                             mask_f[:, b:b + 1, :].broadcast_to([P, C, T]), ALU.add))
                link(nc.vector.tensor_reduce(rmax[:], rho[:], X, ALU.max))
                nc.vector.tensor_tensor(rho[:], rho[:], rmax[:].unsqueeze(2).broadcast_to([P, C, T]),
                                        ALU.subtract).then_inc(v["exp_in"], 1)
                dve.wait_ge(a["att"], b + 1)
                for i in range(2):
                    last = nc.vector.tensor_tensor(
                        att[:, 1 + i], att[:, 0],
                        cwcb[:, i, b * T:(b + 1) * T].unsqueeze(1).broadcast_to([P, C, T]), ALU.mult)
                link(last)
                link(nc.vector.tensor_reduce(sums[:].rearrange("p k c -> p (k c)"),
                                             att[:].rearrange("p k c t -> p (k c) t"), X, ALU.add))
                link(nc.vector.reciprocal(rden[:], sums[:, 0, :]))
                nc.vector.tensor_tensor(wsbs_pre[:], sums[:, 1:3, :],
                                        rden[:].unsqueeze(1).broadcast_to([P, 2, C]), ALU.mult)\
                    .then_inc(v["wsbs_pre"], 1)
                dve.wait_ge(a["wsbs"], b + 1)
                for c in range(C):
                    last = nc.vector.tensor_scalar(nrm[:, b, c, :], h1[:, b, c, :], wsbs[:, 0, c:c + 1],
                                                   wsbs[:, 1, c:c + 1], ALU.mult, ALU.add)
                link(last)
                link(nc.vector.tensor_tensor(x2[:], nrm[:, b], x1[:, b], ALU.add))
                layer_norm(("ffn", b), x2, h2, v["h2"])
                dve.wait_ge(t["gate"], b + 1)
                link(nc.vector.tensor_tensor(logits[:], R[:, 0:C * E].rearrange("p (c e) -> p c e", c=C),
                                             small[:, 0:E].unsqueeze(1).broadcast_to([P, C, E]), ALU.add))
                for c in range(C):
                    last = nc.vector.max(top[:, c, :], logits[:, c, :])
                link(last)
                nc.vector.tensor_tensor(dtop[:], top[:, :, 1], top[:, :, 0], ALU.subtract)\
                    .then_inc(v["dtop"], 1)
                for c in range(C):
                    last = nc.vector.max_index(top_i[:, c, :], top[:, c, :], logits[:, c, :])
                link(last)
                link(nc.vector.tensor_copy(top_f[:], top_i[:]))
                dve.wait_ge(a["etop"], b + 1)
                link(nc.vector.tensor_scalar(p2[:], etop[:], 1.0, None, ALU.add))
                link(nc.vector.reciprocal(p1[:], p2[:]))
                link(nc.vector.tensor_tensor(p2[:], etop[:], p1[:], ALU.mult))
                for c in range(C):
                    nc.vector.tensor_scalar(we1[:, c, :], expert_id[:], top_f[:, c, 0:1], p1[:, c:c + 1],
                                            ALU.is_equal, ALU.mult)
                    last = nc.vector.tensor_scalar(we[:, b, c, :], expert_id[:], top_f[:, c, 1:2],
                                                   p2[:, c:c + 1], ALU.is_equal, ALU.mult)
                link(last)
                nc.vector.tensor_tensor(we[:, b], we[:, b], we1[:], ALU.add).then_inc(v["we"], 1)
                dve.wait_ge(t["weT"], b + 1)
                nc.vector.tensor_copy(weT[:], R[0:E, :]).then_inc(v["weT"], 1)
                dve.wait_ge(t["b3"], b + 1)
                nc.vector.tensor_tensor(acc[:, b], R[:, :].rearrange("p (c d) -> p c d", c=C), x2[:],
                                        ALU.add).then_inc(v["rho_read"], 2)

            def glu(b, step, h):
                n = expert_no(b, step, h)
                e = step * EXPERTS_PER_STEP + h
                for c in range(FC):
                    dve.wait_ge(a["x2b"], FC * n + c + 1)
                    nc.vector.scalar_tensor_tensor(out=z[:, c, :], in0=bank[2 * c][:, :],
                                                   scalar=cols[:, bass.ds(FC * e + c, 1)],
                                                   in1=x2b[:, c, :], op0=ALU.add, op1=ALU.mult)\
                        .then_inc(v["z"], 1)

            def accumulate(b, step, h):
                n = expert_no(b, step, h)
                e = step * EXPERTS_PER_STEP + h
                dve.wait_ge(t["y"], n + 1)
                dve.wait_ge(v["acc"], n)
                for c in range(C):
                    last = nc.vector.scalar_tensor_tensor(out=acc[:, b, c, :],
                                                          in0=bank[6][:, c * P:(c + 1) * P],
                                                          scalar=we[:, b, c, bass.ds(e, 1)],
                                                          in1=acc[:, b, c, :], op0=ALU.mult, op1=ALU.add)
                last.then_inc(v["acc"], 1)

            dve.wait_ge(x_in[0], 16)
            layer_norm(("in", 0), x_sb[:, 0:C], h0[:, 0], v["h0"])
            dve.wait_ge(x_in[1], 16)
            layer_norm(("in", 1), x_sb[:, C:2 * C], h0[:, 1], v["h0"])
            dve.wait_ge(t["cols"], 1)
            nc.vector.tensor_copy(cols[:], bank[7][:, 0:NROWS])
            nc.vector.tensor_copy(ctxT[:], bank[7][:, NROWS:NROWS + B * T])
            nc.vector.tensor_copy(WvT[:], bank[7][:, 256:384]).then_inc(v["cols"], 1)
            dve.wait_ge(t["WvWo"], 1)
            nc.vector.tensor_copy(WvWo[:], bank[6][:, 0:P]).then_inc(v["WvWo"], 1)
            dve.wait_ge(t["txt"], 1)
            nc.vector.tensor_copy(txtT[:], bank[7][:, 0:B * T])
            nc.vector.tensor_copy(cwcb[:].rearrange("p k t -> p (k t)"), bank[7][:, B * T:3 * B * T])\
                .then_inc(v["txt"], 1)
            dve.wait_ge(small_in, 16 * 6)
            link(nc.vector.tensor_scalar(mask_f[:], mask_i[:], -1.0, 1.0, ALU.mult, ALU.add))
            nc.vector.tensor_scalar(mask_f[:], mask_f[:], NEG, None, ALU.mult)
            dve.wait_ge(consts_ready, 2)
            link(nc.vector.tensor_copy(expert_id[:], expert_i[:]))
            for b in range(B):
                attention(b)
            dve.wait_ge(a["FT"], 1)
            dve.wait_ge(v["txt"], 1)
            add_group(0, None, 0)
            for j in range(PER_STEP):
                add_group(0, 0, j)
            with dve.Fori(1, STEPS) as step:
                for j in range(PER_STEP):
                    add_group(0, step, j)
            cross_end(0)
            for b in range(B):
                more = b + 1 < B
                if more:
                    dve.wait_ge(a["FT"], b + 2)
                    add_group(b + 1, None, 0)
                if b == 0:
                    dve.wait_ge(v["rho_read"], 2)
                with dve.Fori(0, STEPS) as step:
                    if more:
                        add_group(b + 1, step, 0)
                    glu(b, step, 0)
                    if more:
                        add_group(b + 1, step, 1)
                    glu(b, step, 1)
                    accumulate(b, step, 0)
                    if more:
                        add_group(b + 1, step, 2)
                    accumulate(b, step, 1)
                if more:
                    cross_end(b + 1)


_INS = ["x", "ctx_1024", "mask_BxS2_ik0", "L0_attn_Wq", "L0_attn_Wk", "L0_attn_Wv", "L0_attn_Wo",
        "L0_attn_bo", "L0_attn_gamma", "L0_attn_beta", "L0_xattn_Ws", "L0_xattn_W", "L0_xattn_w",
        "L0_xattn_b", "L0_xattn_Wcw", "L0_xattn_bcw", "L0_xattn_Wcb", "L0_xattn_bcb", "L0_ffn_gate_w",
        "L0_ffn_gate_b", "L0_ffn_w1", "L0_ffn_b1", "L0_ffn_w2", "L0_ffn_b2", "L0_ffn_wg", "L0_ffn_bg",
        "L0_ffn_w3", "L0_ffn_b3"]


def kernel(**inputs):
    import numpy as _np
    import concourse.bacc as _bacc
    from concourse import mybir as _mybir
    from concourse.bass_utils import run_bass_kernel_spmd as _run

    nc = _bacc.Bacc("TRN2", target_bir_lowering=False, num_devices=1)
    arrays, args = {}, []
    for name in _INS:
        a = _np.ascontiguousarray(inputs[name])
        arrays[f"in_{name}_dram"] = a
        args.append(nc.dram_tensor(f"in_{name}_dram", a.shape, _mybir.dt.from_np(a.dtype),
                                   kind="ExternalInput").ap())
    out = nc.dram_tensor("out_dram", inputs["x"].shape, _mybir.dt.float32, kind="ExternalOutput").ap()
    decoder_layer_program(nc, *args, out)
    r = _run(nc, [arrays], core_ids=[0])
    return r.results[0]["out_dram"]
```

```python
from contextlib import ExitStack

import concourse.bass as bass
from concourse import mybir

ALU = mybir.AluOpType
ACT = mybir.ActivationFunctionType
F32 = mybir.dt.float32
F32R = mybir.dt.float32r
I32 = mybir.dt.int32
U32 = mybir.dt.uint32
X = mybir.AxisListType.X

P = 128
EPS = 1e-5
NEG = -1e30
PAD = -3e38
ON_POOL = 2
PAIR = 2
STAGES = 9
RING = 3
GROUP = 8


def decoder_layer_program(nc, x, ctx, q_mask, Wq, Wk, Wv, Wo, bo, gamma, beta, Ws, W, w, xb, Wcw, bcw,
                          Wcb, bcb, gate_w, gate_b, w1, b1, w2, b2, wg, bg, w3, b3, out):
    B, L, D = x.shape
    T = ctx.shape[1]
    E, _, FF = w1.shape
    C = L // P
    FC = FF // P
    GROUPS = -(-T // GROUP)
    FIRST = T - (GROUPS - 1) * GROUP
    Q4 = 4
    QT = -(-T // Q4)
    QW = P // Q4
    TP = Q4 * QT
    assert D == P and L == C * P and 0 < FIRST <= GROUP and T % Q4 == 1 and QT <= QW
    LN = {}
    for kind in [(k, b) for b in range(B) for k in ("in", "attn", "x")] + [("ffn", b) for b in range(B)]:
        LN[kind] = len(LN)
    XB, WX, WCW, WCB = 3 * E * FC, 3 * E * FC + 1, 3 * E * FC + 2, 3 * E * FC + 3
    NROWS = 3 * E * FC + 4

    with ExitStack() as stack:
        def sb(name, shape, dt=F32):
            return stack.enter_context(nc.sbuf_tensor(name, shape, dt))

        def sem(name):
            return stack.enter_context(nc.semaphore(name))

        bank = [stack.enter_context(nc.psum_tensor(f"bank{i}", [P, 512], F32)) for i in range(8)]

        x_sb = sb("x_sb", [P, B * C, D])
        ctx_sb = sb("ctx_sb", [T, B, D])
        mask_i = sb("mask_i", [P, B, T], I32)
        wqkvo = sb("wqkvo", [P, 4, D])
        xw = sb("xw", [P, 2, D])
        rows = sb("rows", [NROWS, P])
        ln_rows = sb("ln_rows", [P, 3, D])
        small = sb("small", [P, E + 2])
        gate_sb = sb("gate_sb", [P, E])
        b3_sb = sb("b3_sb", [E, D])
        raw_w = sb("raw_w", [P, PAIR, (2 + FC) * FF])
        w_hi = sb("w_hi", [P, PAIR, (2 + FC) * FF], F32R)
        w_lo = sb("w_lo", [P, PAIR, (2 + FC) * FF], F32R)
        w3_sb = sb("w3_sb", [P, PAIR, FC, D])
        gate_hi = sb("gate_hi", [P, E], F32R)
        gate_lo = sb("gate_lo", [P, E], F32R)
        ident = sb("ident", [P, P])
        expert_i = sb("expert_i", [P, E], I32)
        expert_id = sb("expert_id", [P, E])
        minus_half = sb("minus_half", [P, C])
        cols = sb("cols", [P, NROWS])
        ctxT = sb("ctxT", [P, B * T])
        WvT = sb("WvT", [P, P])
        WvWo = sb("WvWo", [P, P])
        txtT = sb("txtT", [P, B * T])
        cwcb = sb("cwcb", [P, 2, B, Q4, QT])
        mask_f = sb("mask_f", [P, B, Q4, QT])
        w_pad = sb("w_pad", [P, 2 * QW - 1])
        stats = sb("stats", [P, C, 6])
        moments = sb("moments", [P, C, 2])
        var_eps = sb("var_eps", [P, C])
        rstd = sb("rstd", [P, C])
        h0 = sb("h0", [P, B, C, D])
        h0bo = sb("h0bo", [P, B, C, D])
        xbeta = sb("xbeta", [P, B, C, D])
        h0T = sb("h0T", [P, B, L])
        neg_qmax = sb("neg_qmax", [P, B, C])
        qsum = sb("qsum", [P, B, C])
        rq = sb("rq", [P, B, C])
        qE = sb("qE", [P, B, C, D])
        qET = sb("qET", [P, B, L])
        neg_kmax = sb("neg_kmax", [P, B])
        ksum = sb("ksum", [P, B])
        rk = sb("rk", [P, B])
        kET = sb("kET", [P, B, L])
        kE = sb("kE", [P, B, C, D])
        AT = sb("AT", [P, B, P])
        Cm = sb("Cm", [P, B, P])
        res = sb("res", [P, B, C, D])
        nrm = sb("nrm", [P, B, C, D])
        x1 = sb("x1", [P, B, C, D])
        h1 = sb("h1", [P, B, C, D])
        h1T = sb("h1T", [P, B, L])
        FT = sb("FT", [P, B, L])
        ring = sb("ring", [P, RING, GROUP, L])
        rhoT = sb("rhoT", [P, L])
        rho = sb("rho", [P, C, Q4, QT])
        rmax = sb("rmax", [P, C])
        att = sb("att", [P, 3, C, TP])
        sums = sb("sums", [P, 3, C])
        rden = sb("rden", [P, C])
        wsbs_pre = sb("wsbs_pre", [P, 2, C])
        wsbs = sb("wsbs", [P, 2, C])
        x2 = sb("x2", [P, C, D])
        h2 = sb("h2", [P, C, D])
        h2T_hi = sb("h2T_hi", [P, B, L], F32R)
        h2T_lo = sb("h2T_lo", [P, B, L], F32R)
        logits = sb("logits", [P, C, E])
        top = sb("top", [P, C, 8])
        top_i = sb("top_i", [P, C, 8], U32)
        top_f = sb("top_f", [P, C, 8])
        dtop = sb("dtop", [P, C])
        etop = sb("etop", [P, C])
        p1 = sb("p1", [P, C])
        p2 = sb("p2", [P, C])
        we1 = sb("we1", [P, C, E])
        we = sb("we", [P, B, C, E])
        weT = sb("weT", [E, L])
        x2b = sb("x2b", [P, FC, L])
        z = sb("z", [P, FC, L])
        z_hi = sb("z_hi", [P, 2, FC, L], F32R)
        z_lo = sb("z_lo", [P, 2, FC, L], F32R)
        s = sb("s", [P, FC, L])
        acc = sb("acc", [P, B, C, D])

        x_in = [sem(f"x_in{b}") for b in range(B)]
        attn_w_in, ctx_in, rows_in, ln_rows_in, xw_in, small_in, gate_in = (
            sem(n) for n in ("attn_w_in", "ctx_in", "rows_in", "ln_rows_in", "xw_in", "small_in", "gate_in"))
        up_w_in = [sem(f"up_w_in{h}") for h in range(PAIR)]
        gate_w_in = [sem(f"gate_w_in{h}") for h in range(PAIR)]
        w3_in = [sem(f"w3_in{h}") for h in range(PAIR)]
        pool_hi, up_split, wg_split, router_split, pool_added = (
            sem(n) for n in ("pool_hi", "up_split", "wg_split", "router_split", "pool_added"))
        out_stored = sem("out_stored")
        zeroed, ident_ready, consts_ready, rstd_ready, pool_rows = (
            sem(n) for n in ("zeroed", "ident_ready", "consts_ready", "rstd_ready", "pool_rows"))
        chain = sem("vector_chain")
        var_ready = sem("var_ready")
        v = {n: sem("v_" + n) for n in (
            "cols", "WvT", "WvWo", "txt", "h0", "neg_kmax", "neg_qmax", "kE", "AT", "C", "h1", "added",
            "exp_in", "wsbs_pre", "h2", "h2T_lo", "dtop", "we", "weT", "z", "z_lo", "acc", "acc_start")}
        a = {n: sem("a_" + n) for n in (
            "h0T", "kexp", "qexp", "qET", "h1T", "FT", "rhoT", "tanh", "att", "wsbs", "h2T", "etop", "x2b", "z_hi", "silu")}
        t = {n: sem("t_" + n) for n in (
            "cols", "WvWo", "txt", "h0T", "q", "k", "kE", "qET", "AT", "C", "out", "h1T", "FT", "rhoT",
            "rho", "h2T", "gate", "weT", "b3", "x12", "g", "y")}

        block = stack.enter_context(nc.Block())

        def text_group(g):
            b, k = divmod(g, GROUPS)
            return b, FIRST + (k - 1) * GROUP if k else 0, GROUP if k else FIRST, g % RING

        def on_pool(g):
            return ON_POOL if g < GROUPS else {GROUPS + 2: GROUP, GROUPS + 3: GROUP // 2, GROUPS + 4: GROUP}.get(g, 0)

        def pool_groups(g):
            return sum(1 for k in range(g + 1) if on_pool(k))

        def vector_groups(g):
            return sum(1 for k in range(g + 1) if on_pool(k) < text_group(k)[2])

        LATE = GROUPS + 4
        tanh_place = {g: (3 * (g - LATE) + 1) // 2 for g in range(LATE, B * GROUPS)}

        def groups_at(place, shift):
            return [g for g in tanh_place if tanh_place[g] + shift == place and (shift >= 0 or on_pool(g) < GROUP)]

        END = tanh_place[B * GROUPS - 1] + 2
        stages_at = {END: [0], END + 1: [1, 2], END + 3: [3], END + 4: [4], END + 5: [5], 2 * E: [6]}
        assert END + 5 < 2 * E

        def positive(value):
            return not (isinstance(value, int) and value <= 0)

        attention_banks = [bank[0:4], bank[4:7] + [bank[3]]]
        end_bank = [bank[6], bank[7]]

        def following(b, e):
            return (b, e + 1) if e + 1 < E else (b + 1, 0)

        @block.sync
        def _(sp):
            def load_x(b):
                sp.dma_start(x_sb[:, b * C:(b + 1) * C, :],
                             x[b].rearrange("(c p) d -> p c d", p=P)).then_inc(x_in[b], 16)

            load_x(0)
            sp.dma_start(rows[XB:XB + 1, :], xb).then_inc(rows_in, 16)
            sp.dma_start(rows[WX:WX + 1, :], w.rearrange("d o -> o d")).then_inc(rows_in, 16)
            sp.dma_start(rows[WCW:WCW + 1, :], Wcw).then_inc(rows_in, 16)
            sp.dma_start(rows[WCB:WCB + 1, :], Wcb).then_inc(rows_in, 16)
            for i, m in enumerate((b1, b2, bg)):
                sp.dma_start(rows[i * E * FC:(i + 1) * E * FC, :], m.rearrange("e (c p) -> (e c) p", p=P))\
                    .then_inc(rows_in, 16)
            sp.dma_start(ctx_sb[:], ctx.rearrange("b t d -> t b d")).then_inc(ctx_in, 16)
            for i, m in enumerate((bo, gamma, beta)):
                sp.dma_start(ln_rows[:, i, :], m.rearrange("(o d) -> o d", o=1).broadcast_to([P, D]))\
                    .then_inc(ln_rows_in, 16)
            for i, m in enumerate((Ws, W)):
                sp.dma_start(xw[:, i, :], m).then_inc(xw_in, 16)
            for b in range(1, B):
                load_x(b)

            def load_up(e, h):
                sp.dma_start(raw_w[:, h, 0:FF], w1[e]).then_inc(up_w_in[h], 16)
                sp.dma_start(raw_w[:, h, FF:2 * FF], w2[e]).then_inc(up_w_in[h], 16)

            def load_gate(e, h):
                sp.dma_start(raw_w[:, h, 2 * FF:].rearrange("p (k f) -> p k f", k=FC),
                             wg[e].rearrange("(k p) f -> p k f", p=P)).then_inc(gate_w_in[h], 16)

            def load_down(e, h):
                sp.dma_start(w3_sb[:, h, :, :], w3[e].rearrange("(k p) f -> p k f", p=P))\
                    .then_inc(w3_in[h], 16)

            def load_step(n, e, e_before, h):
                sp.wait_ge(up_split, n - 1)
                load_up(e, h)
                sp.wait_ge(wg_split, n - 1)
                load_gate(e, h)
                if positive(n - 2):
                    sp.wait_ge(t["y"], n - 2)
                load_down(e_before, 1 - h)

            for h in range(PAIR):
                load_up(h, h)
                load_gate(h, h)
            load_down(0, 0)
            for b in range(B):
                peeled = PAIR if b == 0 else 0
                for e in range(peeled, peeled + PAIR):
                    load_step(E * b + e, e, (e - 1) % E, e % PAIR)
                with sp.Fori(peeled // PAIR + 1, E // PAIR) as pair:
                    for h in range(PAIR):
                        e = PAIR * pair + h
                        load_step(E * b + e, e, PAIR * pair + h - 1, h)
            sp.wait_ge(t["y"], B * E - 2)
            load_down(E - 1, (B * E - 1) % PAIR)
            for b in range(B):
                sp.wait_ge(v["acc"], E * (b + 1))
                sp.dma_start(out[b].rearrange("(c p) d -> p c d", p=P), acc[:, b, :, :])\
                    .then_inc(out_stored, 16)
            sp.wait_ge(out_stored, 16 * B)

        @block.gpsimd
        def _(pool):
            nc.gpsimd.memset(ident[:], 0.0).then_inc(zeroed, 1)
            nc.gpsimd.memset(minus_half[:], -0.5).then_inc(consts_ready, 1)
            nc.gpsimd.iota(expert_i[:], pattern=[[1, E]], base=0, channel_multiplier=0)\
                .then_inc(consts_ready, 1)
            pool.wait_ge(zeroed, 1)
            nc.gpsimd.affine_select(out=ident[:], in_=ident[:], compare_op=ALU.not_equal, fill=1.0, base=0,
                                    pattern=[[-1, P]], channel_multiplier=1).then_inc(ident_ready, 1)
            pool.wait_ge(consts_ready, 2)

            def add_group(g):
                b, t0, n, slot = text_group(g)
                if g >= RING:
                    pool.wait_ge(t["rho"], g - RING + 1)
                for i in range(n - on_pool(g), n):
                    last = nc.gpsimd.tensor_scalar(ring[:, slot, i, :], FT[:, b, :],
                                                   txtT[:, b * T + t0 + i:b * T + t0 + i + 1], 1.0,
                                                   ALU.add, ALU.mult)
                last.then_inc(pool_added, 1)

            def rstd_of():
                nonlocal ln
                pool.wait_ge(var_ready, ln + 1)
                nc.gpsimd.tensor_tensor(rstd[:], var_eps[:], minus_half[:], ALU.pow)\
                    .then_inc(rstd_ready, 1)
                ln += 1

            def attention_rows(b):
                pool.wait_ge(ln_rows_in, 16 * 3)
                pool.wait_ge(v["h0"], b + 1)
                nc.gpsimd.tensor_tensor(h0bo[:, b], h0[:, b],
                                        ln_rows[:, 0:1, :].broadcast_to([P, C, D]), ALU.add)\
                    .then_inc(pool_rows, 1)
                nc.gpsimd.tensor_tensor(xbeta[:, b], x_sb[:, b * C:(b + 1) * C, :],
                                        ln_rows[:, 2:3, :].broadcast_to([P, C, D]), ALU.add)\
                    .then_inc(pool_rows, 1)

            splits = 0

            def split(hi, lo, src, done):
                nonlocal splits
                splits += 1
                nc.gpsimd.tensor_scalar(hi, src, 0.0, 1.0, ALU.add, ALU.mult).then_inc(pool_hi, 1)
                pool.wait_ge(pool_hi, splits)
                nc.gpsimd.tensor_tensor(lo, src, hi.bitcast(F32), ALU.subtract).then_inc(done, 1)

            def split_up(n):
                h = n % PAIR
                pool.wait_ge(up_w_in[h], 32 * (n // PAIR + 1))
                if positive(n - 1):
                    pool.wait_ge(t["x12"], FC * (n - 1))
                split(w_hi[:, h, 0:2 * FF], w_lo[:, h, 0:2 * FF], raw_w[:, h, 0:2 * FF], up_split)

            def split_wg(n):
                h = n % PAIR
                pool.wait_ge(gate_w_in[h], 16 * (n // PAIR + 1))
                if positive(n - 1):
                    pool.wait_ge(t["g"], FC * (n - 1))
                split(w_hi[:, h, 2 * FF:], w_lo[:, h, 2 * FF:], raw_w[:, h, 2 * FF:], wg_split)

            ln = 0
            rstd_of()
            nc.gpsimd.dma_start(mask_i[:], q_mask.rearrange("(o b) t -> o b t", o=1)
                                .broadcast_to([P, B, T])).then_inc(small_in, 16)
            attention_rows(0)
            nc.gpsimd.dma_start(small[:, E:E + 1], bcw.rearrange("(o e) -> o e", o=1).broadcast_to([P, 1]))\
                .then_inc(small_in, 16)
            nc.gpsimd.dma_start(small[:, E + 1:E + 2], bcb.rearrange("(o e) -> o e", o=1)
                                .broadcast_to([P, 1])).then_inc(small_in, 16)
            nc.gpsimd.dma_start(gate_sb[:], gate_w).then_inc(gate_in, 16)
            nc.gpsimd.dma_start(small[:, 0:E], gate_b.rearrange("(o e) -> o e", o=1).broadcast_to([P, E]))\
                .then_inc(gate_in, 16)
            nc.gpsimd.dma_start(b3_sb[:], b3).then_inc(gate_in, 16)
            rstd_of()
            rstd_of()
            rstd_of()
            attention_rows(1)
            pool.wait_ge(gate_in, 48)
            split(gate_hi[:], gate_lo[:], gate_sb[:], router_split)
            pool.wait_ge(a["FT"], 1)
            pool.wait_ge(v["txt"], 1)
            add_group(0)
            add_group(1)
            for g in range(GROUPS):
                if g + 2 < GROUPS:
                    add_group(g + 2)
                if g + 1 in (5, 7):
                    rstd_of()
                if g == 2:
                    split_up(0)
                if g == 3:
                    split_wg(0)
                if g == 4:
                    split_up(1)
            pool.wait_ge(a["FT"], 2)
            add_group(GROUPS + 2)
            add_group(GROUPS + 3)
            rstd_of()
            for n in range(1, B * E):
                if n == (END + 1) // 2 + 2:
                    rstd_of()
                split_wg(n)
                if n == 1:
                    add_group(LATE)
                if n + 1 < B * E:
                    split_up(n + 1)

        @block.scalar
        def _(act):
            for i in (1, 0, 2, 3):
                act.dma_start(wqkvo[:, i, :], (Wq, Wk, Wv, Wo)[i]).then_inc(attn_w_in, 16)

            def attention(b, stage):
                A, Q, K, M = attention_banks[b]
                if stage == 1:
                    act.wait_ge(t["h0T"], b + 1)
                    nc.scalar.copy(h0T[:, b, :], A[:, :]).then_inc(a["h0T"], 1)
                if stage == 2:
                    act.wait_ge(t["k"], b + 1)
                    act.wait_ge(v["neg_kmax"], b + 1)
                    nc.scalar.activation(kET[:, b, :], K[:, :], ACT.Exp, bias=neg_kmax[:, b:b + 1],
                                         accum_out=ksum[:, b:b + 1]).then_inc(a["kexp"], 1)
                    act.wait_ge(v["neg_qmax"], b + 1)
                    for c in range(C):
                        nc.scalar.activation(qE[:, b, c, :], Q[:, c * P:(c + 1) * P], ACT.Exp,
                                             bias=neg_qmax[:, b, c:c + 1],
                                             accum_out=qsum[:, b, c:c + 1]).then_inc(a["qexp"], 1)
                if stage == 3:
                    act.wait_ge(t["qET"], b + 1)
                    nc.scalar.copy(qET[:, b, :], Q[:, :]).then_inc(a["qET"], 1)
                if stage == 8:
                    act.wait_ge(t["h1T"], b + 1)
                    nc.scalar.copy(h1T[:, b, :], M[:, :]).then_inc(a["h1T"], 1)
                    act.wait_ge(t["FT"], b + 1)
                    if b == 0:
                        act.wait_ge(v["cols"], 1)
                        act.wait_ge(small_in, 16 * 3)
                    nc.scalar.activation(FT[:, b, :], A[:, :], ACT.Identity, bias=cols[:, XB:XB + 1])\
                        .then_inc(a["FT"], 1)

            def tanh_group(g):
                _, _, n, slot = text_group(g)
                if on_pool(g) < n:
                    act.wait_ge(v["added"], vector_groups(g))
                if on_pool(g):
                    act.wait_ge(pool_added, pool_groups(g))
                nc.scalar.activation(ring[:, slot, 0:n, :], ring[:, slot, 0:n, :], ACT.Tanh)\
                    .then_inc(a["tanh"], 1)

            def cross_end(b, stage):
                if stage == 0:
                    act.wait_ge(t["rho"], GROUPS * (b + 1))
                    nc.scalar.copy(rhoT[:], bank[7][:, :]).then_inc(a["rhoT"], 1)
                if stage == 1:
                    act.wait_ge(v["exp_in"], b + 1)
                    nc.scalar.activation(att[:, 0, :, :], rho[:].rearrange("p c q i -> p c (q i)"),
                                         ACT.Exp).then_inc(a["att"], 1)
                    act.wait_ge(v["wsbs_pre"], b + 1)
                    nc.scalar.activation(wsbs[:, 0, :], wsbs_pre[:, 0, :], ACT.Tanh, bias=small[:, E:E + 1])
                    nc.scalar.activation(wsbs[:, 1, :], wsbs_pre[:, 1, :], ACT.Tanh,
                                         bias=small[:, E + 1:E + 2]).then_inc(a["wsbs"], 1)
                if stage == 3:
                    act.wait_ge(t["h2T"], b + 1)
                    nc.scalar.copy(h2T_hi[:, b, :], end_bank[b][:, :]).then_inc(a["h2T"], 1)
                if stage == 4:
                    act.wait_ge(v["dtop"], b + 1)
                    nc.scalar.activation(etop[:], dtop[:], ACT.Exp).then_inc(a["etop"], 1)

            def glu_part(b, e, h):
                n = E * b + e
                for c in range(FC):
                    act.wait_ge(t["x12"], FC * n + c + 1)
                    if positive(FC * (n - 1) + c + 1):
                        act.wait_ge(v["z"], FC * (n - 1) + c + 1)
                    nc.scalar.activation(x2b[:, c, :], bank[2 * c + 1][:, :], ACT.Identity,
                                         bias=cols[:, bass.ds(E * FC + FC * e + c, 1)]).then_inc(a["x2b"], 1)
                for c in range(FC):
                    act.wait_ge(v["z"], FC * n + c + 1)
                    if positive(n - 1):
                        act.wait_ge(t["g"], FC * (n - 1))
                    nc.scalar.copy(z_hi[:, h, c, :], z[:, c, :]).then_inc(a["z_hi"], 1)

            def silu_part(b, e):
                n = E * b + e
                for c in range(FC):
                    act.wait_ge(t["g"], FC * n + c + 1)
                    nc.scalar.activation(s[:, c, :], bank[4 + c][:, :], ACT.Silu,
                                         bias=cols[:, bass.ds(2 * E * FC + FC * e + c, 1)])\
                        .then_inc(a["silu"], 1)

            for stage in range(STAGES):
                attention(0, stage)
            tanh_group(0)
            for g in range(GROUPS):
                if g + 1 < GROUPS:
                    tanh_group(g + 1)
                attention(1, g + 1)
            cross_end(0, 0)
            tanh_group(GROUPS)
            cross_end(0, 1)
            tanh_group(GROUPS + 1)
            tanh_group(GROUPS + 2)
            cross_end(0, 3)
            tanh_group(GROUPS + 3)
            glu_part(0, 0, 0)
            cross_end(0, 4)
            def between(place):
                for g in groups_at(place, 0):
                    tanh_group(g)
                for stage in stages_at.get(place, []):
                    cross_end(1, stage)

            for e in range(E):
                between(2 * e)
                glu_part(*following(0, e), (e + 1) % PAIR)
                between(2 * e + 1)
                silu_part(0, e)
            glu_part(1, 1, 1)
            silu_part(1, 0)
            with act.Fori(0, E // PAIR - 1) as pair:
                for h in range(PAIR):
                    glu_part(1, PAIR * pair + 2 + h, h)
                    silu_part(1, PAIR * pair + 1 + h)
            silu_part(1, E - 1)

        @block.tensor
        def _(pe):
            def transposed(out_ap, in_ap, k):
                return nc.tensor.transpose(out_ap, in_ap, ident[0:k, 0:k])

            def exact_product(acc_ap, operands):
                parts = [x for l_hi, l_lo, r_hi, r_lo in operands
                         for x in ((l_hi, r_hi), (l_hi, r_lo), (l_lo, r_hi))]
                for i, (lhsT, rhs) in enumerate(parts):
                    mm = nc.tensor.matmul(acc_ap, lhsT, rhs, start=(i == 0), stop=(i == len(parts) - 1))
                return mm

            def attention(b, stage):
                A, Q, K, M = attention_banks[b]
                if stage == 1:
                    pe.wait_ge(v["h0"], b + 1)
                    for c in range(C):
                        mm = transposed(A[:, c * P:(c + 1) * P], h0[:, b, c, :], P)
                    mm.then_inc(t["h0T"], 1)
                    pe.wait_ge(a["h0T"], b + 1)
                    nc.tensor.matmul(K[:, :], wqkvo[:, 1, :], h0T[:, b, :], start=True, stop=True)\
                        .then_inc(t["k"], 1)
                    for c in range(C):
                        mm = nc.tensor.matmul(Q[:, c * P:(c + 1) * P], h0T[:, b, c * P:(c + 1) * P],
                                              wqkvo[:, 0, :], start=True, stop=True)
                    mm.then_inc(t["q"], 1)
                if stage == 3:
                    pe.wait_ge(a["kexp"], b + 1)
                    for c in range(C):
                        mm = transposed(A[:, c * P:(c + 1) * P], kET[:, b, c * P:(c + 1) * P], P)
                    mm.then_inc(t["kE"], 1)
                    pe.wait_ge(a["qexp"], C * (b + 1))
                    for c in range(C):
                        mm = transposed(Q[:, c * P:(c + 1) * P], qE[:, b, c, :], P)
                    mm.then_inc(t["qET"], 1)
                if stage == 4:
                    pe.wait_ge(v["kE"], b + 1)
                    for c in range(C):
                        mm = nc.tensor.matmul(K[:, 0:P], h0[:, b, c, :], kE[:, b, c, :],
                                              start=(c == 0), stop=(c == C - 1))
                    mm.then_inc(t["AT"], 1)
                    pe.wait_ge(v["AT"], b + 1)
                    nc.tensor.matmul(K[:, P:2 * P], AT[:, b, :], WvWo[:], start=True, stop=True)\
                        .then_inc(t["C"], 1)
                if stage == 5:
                    pe.wait_ge(a["qET"], b + 1)
                    pe.wait_ge(v["C"], b + 1)
                    for c in range(C):
                        mm = nc.tensor.matmul(A[:, c * P:(c + 1) * P], qET[:, b, c * P:(c + 1) * P],
                                              Cm[:, b, :], start=True, stop=True)
                    mm.then_inc(t["out"], 1)
                if stage == 8:
                    pe.wait_ge(v["h1"], b + 1)
                    for c in range(C):
                        mm = transposed(M[:, c * P:(c + 1) * P], h1[:, b, c, :], P)
                    mm.then_inc(t["h1T"], 1)
                    pe.wait_ge(a["h1T"], b + 1)
                    nc.tensor.matmul(A[:, :], xw[:, 1, :], h1T[:, b, :], start=True, stop=True)\
                        .then_inc(t["FT"], 1)

            def score_group(g):
                b, t0, n, slot = text_group(g)
                pe.wait_ge(a["tanh"], g + 1)
                if b and t0 == 0:
                    pe.wait_ge(a["rhoT"], b)
                for i in range(n):
                    q, row = (t0 + i) % Q4, (t0 + i) // Q4
                    mm = nc.tensor.matmul(bank[7][q * QW:(q + 1) * QW, :],
                                          w_pad[:, QW - 1 - row:2 * QW - 1 - row],
                                          ring[:, slot, i, :], start=(row == 0),
                                          stop=(t0 + i + Q4 >= T))
                mm.then_inc(t["rho"], 1)

            def cross_end(b, stage):
                R = end_bank[b]
                if stage == 0:
                    pe.wait_ge(a["rhoT"], b + 1)
                    for c in range(C):
                        mm = transposed(R[:, c * P:(c + 1) * P], rhoT[:, c * P:(c + 1) * P], P)
                    mm.then_inc(t["rhoT"], 1)
                if stage == 3:
                    pe.wait_ge(v["h2"], b + 1)
                    for c in range(C):
                        mm = transposed(R[:, c * P:(c + 1) * P], h2[:, c, :], P)
                    mm.then_inc(t["h2T"], 1)
                if stage == 4:
                    pe.wait_ge(a["h2T"], b + 1)
                    pe.wait_ge(v["h2T_lo"], b + 1)
                    pe.wait_ge(router_split, 1)
                    for c in range(C):
                        col = slice(c * P, (c + 1) * P)
                        mm = exact_product(R[:, c * E:(c + 1) * E],
                                           [(h2T_hi[:, b, col], h2T_lo[:, b, col], gate_hi[:], gate_lo[:])])
                    mm.then_inc(t["gate"], 1)
                if stage == 5:
                    pe.wait_ge(v["we"], b + 1)
                    for c in range(C):
                        mm = transposed(R[0:E, c * P:(c + 1) * P], we[:, b, c, :], P)
                    mm.then_inc(t["weT"], 1)
                if stage == 6:
                    pe.wait_ge(v["weT"], b + 1)
                    for c in range(C):
                        mm = nc.tensor.matmul(R[:, c * P:(c + 1) * P], weT[:, c * P:(c + 1) * P],
                                              b3_sb[:], start=True, stop=True)
                    mm.then_inc(t["b3"], 1)

            def expert_up(b, e, h):
                n = E * b + e
                pe.wait_ge(up_split, n + 1)
                if not positive(e):
                    pe.wait_ge(a["h2T"], b + 1)
                    pe.wait_ge(v["h2T_lo"], b + 1)
                for c in range(FC):
                    if positive(FC * (n - 1) + c + 1):
                        pe.wait_ge(v["z"], FC * (n - 1) + c + 1)
                    for i in range(2):
                        col = slice(i * FF + c * P, i * FF + (c + 1) * P)
                        mm = exact_product(bank[2 * c + i][:, :], [(w_hi[:, h, col], w_lo[:, h, col],
                                                                    h2T_hi[:, b, :], h2T_lo[:, b, :])])
                    mm.then_inc(t["x12"], 1)

            def expert_gate(b, e, h):
                n = E * b + e
                for c in range(FC):
                    if positive(FC * (n - 1) + c + 1):
                        pe.wait_ge(a["silu"], FC * (n - 1) + c + 1)
                    if c == 0:
                        pe.wait_ge(wg_split, n + 1)
                        pe.wait_ge(v["z_lo"], FC * n + FC)
                    cols_of = [slice((2 + k) * FF + c * P, (2 + k) * FF + (c + 1) * P) for k in range(FC)]
                    exact_product(bank[4 + c][:, :], [(w_hi[:, h, col], w_lo[:, h, col],
                                                       z_hi[:, h, k, :], z_lo[:, h, k, :])
                                                      for k, col in enumerate(cols_of)])\
                        .then_inc(t["g"], 1)

            def expert_down(b, e, h, turn):
                n = E * b + e
                pe.wait_ge(w3_in[h], 16 * (turn + 1))
                pe.wait_ge(a["silu"], FC * n + FC)
                if positive(n):
                    pe.wait_ge(v["acc"], n)
                else:
                    pe.wait_ge(v["acc_start"], 1)
                for c in range(C):
                    for k in range(FC):
                        mm = nc.tensor.matmul(bank[6][:, c * P:(c + 1) * P], s[:, k, c * P:(c + 1) * P],
                                              w3_sb[:, h, k, :], start=(k == 0), stop=(k == FC - 1))
                mm.then_inc(t["y"], 1)

            pe.wait_ge(ident_ready, 1)
            pe.wait_ge(attn_w_in, 64)
            attention(0, 1)
            transposed(bank[7][:, 256:384], wqkvo[:, 2, :], P)
            pe.wait_ge(rows_in, 16 * 7)
            transposed(bank[7][:, 0:NROWS], rows[:], NROWS)
            pe.wait_ge(ctx_in, 16)
            for b in range(B):
                mm = transposed(bank[7][:, NROWS + b * T:NROWS + (b + 1) * T], ctx_sb[:, b, :], T)
            mm.then_inc(t["cols"], 1)
            attention(0, 3)
            pe.wait_ge(v["cols"], 1)
            nc.tensor.matmul(bank[6][:, 0:P], WvT[:], wqkvo[:, 3, :], start=True, stop=True)\
                .then_inc(t["WvWo"], 1)
            pe.wait_ge(v["WvWo"], 1)
            attention(0, 4)
            attention(0, 5)
            pe.wait_ge(xw_in, 32)
            nc.tensor.matmul(bank[7][:, 0:B * T], xw[:, 0, :], ctxT[:], start=True, stop=True)
            for i, col in enumerate((WCW, WCB)):
                mm = nc.tensor.matmul(bank[7][:, (1 + i) * B * T:(2 + i) * B * T],
                                      cols[:, col:col + 1].broadcast_to([P, P]), ctxT[:],
                                      start=True, stop=True)
            mm.then_inc(t["txt"], 1)
            attention(0, 8)
            pe.wait_ge(v["txt"], 1)
            for g in range(GROUPS):
                score_group(g)
                attention(1, g + 1)
            cross_end(0, 0)
            score_group(GROUPS)
            score_group(GROUPS + 1)
            cross_end(0, 3)
            expert_up(0, 0, 0)
            cross_end(0, 4)
            score_group(GROUPS + 2)

            def between(place):
                for g in groups_at(place, 2):
                    score_group(g)
                for stage in stages_at.get(place, []):
                    cross_end(1, stage)

            for e in range(E):
                between(2 * e)
                expert_up(*following(0, e), (e + 1) % PAIR)
                if e:
                    expert_down(0, e - 1, (e - 1) % PAIR, (e - 1) // PAIR)
                if e == 0:
                    cross_end(0, 5)
                between(2 * e + 1)
                expert_gate(0, e, e % PAIR)
                if e == 0:
                    cross_end(0, 6)
                    score_group(GROUPS + 3)
            between(2 * E)
            expert_up(1, 1, 1)
            expert_down(0, E - 1, 1, E // PAIR - 1)
            expert_gate(1, 0, 0)
            with pe.Fori(0, E // PAIR - 1) as pair:
                for h in range(PAIR):
                    expert_up(1, PAIR * pair + 2 + h, h)
                    expert_down(1, PAIR * pair + h, h, pair + E // PAIR)
                    expert_gate(1, PAIR * pair + 1 + h, 1 - h)
            expert_down(1, E - 2, 0, B * E // PAIR - 1)
            expert_gate(1, E - 1, 1)
            expert_down(1, E - 1, 1, B * E // PAIR - 1)

        @block.vector
        def _(dve):
            links = 0

            def link(ins):
                nonlocal links
                links += 1
                ins.then_inc(chain, 1)
                dve.wait_ge(chain, links)

            def norm_stats(src):
                for c in range(C):
                    last = nc.vector.bn_stats(stats[:, c, :], src[:, c, :])
                link(last)
                for c in range(C):
                    last = nc.vector.bn_aggr(moments[:, c, :], stats[:, c, :])
                link(last)
                nc.vector.tensor_scalar(var_eps[:], moments[:, :, 1], EPS, None, ALU.add)\
                    .then_inc(var_ready, 1)

            def norm_apply(which, src, dst):
                dve.wait_ge(rstd_ready, LN[which] + 1)
                for c in range(C):
                    last = nc.vector.tensor_scalar(dst[:, c, :], src[:, c, :], moments[:, c, 0:1],
                                                   rstd[:, c:c + 1], ALU.subtract, ALU.mult)
                return last

            def attention(b, stage):
                A, Q, K, M = attention_banks[b]
                xs = x_sb[:, b * C:(b + 1) * C]
                if stage == 0:
                    dve.wait_ge(x_in[b], 16)
                    norm_stats(xs)
                    norm_apply(("in", b), xs, h0[:, b]).then_inc(v["h0"], 1)
                if stage == 2:
                    dve.wait_ge(t["k"], b + 1)
                    nc.vector.tensor_reduce(neg_kmax[:, b:b + 1], K[:, :], X, ALU.max, negate=True)\
                        .then_inc(v["neg_kmax"], 1)
                    dve.wait_ge(t["q"], b + 1)
                    nc.vector.tensor_reduce(neg_qmax[:, b, :], Q[:, :].rearrange("p (c d) -> p c d", c=C),
                                            X, ALU.max, negate=True).then_inc(v["neg_qmax"], 1)
                if stage == 3:
                    dve.wait_ge(t["kE"], b + 1)
                    nc.vector.tensor_copy(kE[:, b].rearrange("p c d -> p (c d)"), A[:, :])\
                        .then_inc(v["kE"], 1)
                if stage == 4:
                    dve.wait_ge(a["kexp"], b + 1)
                    nc.vector.reciprocal(rk[:, b:b + 1], ksum[:, b:b + 1])
                    dve.wait_ge(a["qexp"], C * (b + 1))
                    link(nc.vector.reciprocal(rq[:, b, :], qsum[:, b, :]))
                    dve.wait_ge(t["AT"], b + 1)
                    nc.vector.tensor_copy(AT[:, b, :], K[:, 0:P]).then_inc(v["AT"], 1)
                    dve.wait_ge(t["C"], b + 1)
                    nc.vector.tensor_scalar(Cm[:, b, :], K[:, P:2 * P], rk[:, b:b + 1], float(D) ** -0.5,
                                            ALU.mult, ALU.mult).then_inc(v["C"], 1)
                if stage == 5:
                    dve.wait_ge(t["out"], b + 1)
                    dve.wait_ge(pool_rows, 2 * (b + 1))
                    for c in range(C):
                        last = nc.vector.scalar_tensor_tensor(
                            out=res[:, b, c, :], in0=A[:, c * P:(c + 1) * P], scalar=rq[:, b, c:c + 1],
                            in1=h0bo[:, b, c, :], op0=ALU.mult, op1=ALU.add)
                    link(last)
                    norm_stats(res[:, b])
                if stage == 6:
                    link(norm_apply(("attn", b), res[:, b], nrm[:, b]))
                    link(nc.vector.tensor_tensor(nrm[:, b], nrm[:, b],
                                                 ln_rows[:, 1:2, :].broadcast_to([P, C, D]), ALU.mult))
                    link(nc.vector.tensor_tensor(x1[:, b], nrm[:, b], xbeta[:, b], ALU.add))
                if stage == 7:
                    norm_stats(x1[:, b])
                if stage == 8:
                    norm_apply(("x", b), x1[:, b], h1[:, b]).then_inc(v["h1"], 1)

            def add_group(g):
                b, t0, n, slot = text_group(g)
                if g >= RING:
                    dve.wait_ge(t["rho"], g - RING + 1)
                for i in range(n - on_pool(g)):
                    last = nc.vector.tensor_scalar(ring[:, slot, i, :], FT[:, b, :],
                                                   txtT[:, b * T + t0 + i:b * T + t0 + i + 1], None, ALU.add)
                last.then_inc(v["added"], 1)

            def cross_end(b, stage):
                R = end_bank[b]
                if stage == 0:
                    dve.wait_ge(t["rhoT"], b + 1)
                    if b > 0:
                        dve.wait_ge(a["att"], b)
                    link(nc.vector.tensor_tensor(
                        rho[:], R[:, :].rearrange("p (c q i) -> p c q i", c=C, q=Q4)[:, :, :, 0:QT],
                        mask_f[:, b].unsqueeze(1).broadcast_to([P, C, Q4, QT]), ALU.add))
                    r = rho[:].rearrange("p c q i -> p c (q i)")
                    link(nc.vector.tensor_reduce(rmax[:], r, X, ALU.max))
                    nc.vector.tensor_tensor(r, r, rmax[:].unsqueeze(2).broadcast_to([P, C, TP]),
                                            ALU.subtract).then_inc(v["exp_in"], 1)
                if stage == 1:
                    dve.wait_ge(a["att"], b + 1)
                    for i in range(2):
                        last = nc.vector.tensor_tensor(
                            att[:, 1 + i], att[:, 0],
                            cwcb[:, i, b].rearrange("p q i -> p (q i)").unsqueeze(1)
                            .broadcast_to([P, C, TP]), ALU.mult)
                    link(last)
                    link(nc.vector.tensor_reduce(sums[:].rearrange("p k c -> p (k c)"),
                                                 att[:].rearrange("p k c t -> p (k c) t"), X, ALU.add))
                    link(nc.vector.reciprocal(rden[:], sums[:, 0, :]))
                    nc.vector.tensor_tensor(wsbs_pre[:], sums[:, 1:3, :],
                                            rden[:].unsqueeze(1).broadcast_to([P, 2, C]), ALU.mult)\
                        .then_inc(v["wsbs_pre"], 1)
                if stage == 2:
                    dve.wait_ge(a["wsbs"], b + 1)
                    for c in range(C):
                        last = nc.vector.tensor_scalar(nrm[:, b, c, :], h1[:, b, c, :],
                                                       wsbs[:, 0, c:c + 1], wsbs[:, 1, c:c + 1],
                                                       ALU.mult, ALU.add)
                    link(last)
                    link(nc.vector.tensor_tensor(x2[:], nrm[:, b], x1[:, b], ALU.add))
                    norm_stats(x2)
                if stage == 3:
                    norm_apply(("ffn", b), x2, h2).then_inc(v["h2"], 1)
                    if b == 0:
                        add_group(GROUPS + 3)
                    dve.wait_ge(a["h2T"], b + 1)
                    nc.vector.tensor_tensor(h2T_lo[:, b, :], R[:, :], h2T_hi[:, b, :].bitcast(F32),
                                            ALU.subtract).then_inc(v["h2T_lo"], 1)
                if stage == 4:
                    dve.wait_ge(t["gate"], b + 1)
                    link(nc.vector.tensor_tensor(
                        logits[:], R[:, 0:C * E].rearrange("p (c e) -> p c e", c=C),
                        small[:, 0:E].unsqueeze(1).broadcast_to([P, C, E]), ALU.add))
                    for c in range(C):
                        last = nc.vector.max(top[:, c, :], logits[:, c, :])
                    link(last)
                    nc.vector.tensor_tensor(dtop[:], top[:, :, 1], top[:, :, 0], ALU.subtract)\
                        .then_inc(v["dtop"], 1)
                    for c in range(C):
                        last = nc.vector.max_index(top_i[:, c, :], top[:, c, :], logits[:, c, :])
                    link(last)
                    link(nc.vector.tensor_copy(top_f[:], top_i[:]))
                    dve.wait_ge(a["etop"], b + 1)
                    link(nc.vector.tensor_scalar(p2[:], etop[:], 1.0, None, ALU.add))
                    link(nc.vector.reciprocal(p1[:], p2[:]))
                    link(nc.vector.tensor_tensor(p2[:], etop[:], p1[:], ALU.mult))
                    for c in range(C):
                        nc.vector.tensor_scalar(we1[:, c, :], expert_id[:], top_f[:, c, 0:1],
                                                p1[:, c:c + 1], ALU.is_equal, ALU.mult)
                        last = nc.vector.tensor_scalar(we[:, b, c, :], expert_id[:], top_f[:, c, 1:2],
                                                       p2[:, c:c + 1], ALU.is_equal, ALU.mult)
                    link(last)
                    nc.vector.tensor_tensor(we[:, b], we[:, b], we1[:], ALU.add).then_inc(v["we"], 1)
                if stage == 5:
                    dve.wait_ge(t["weT"], b + 1)
                    nc.vector.tensor_copy(weT[:], R[0:E, :]).then_inc(v["weT"], 1)
                if stage == 6:
                    dve.wait_ge(t["b3"], b + 1)
                    nc.vector.tensor_tensor(acc[:, b], R[:, :].rearrange("p (c d) -> p c d", c=C), x2[:],
                                            ALU.add).then_inc(v["acc_start"], 1)
                    dve.wait_ge(v["acc_start"], b + 1)

            def glu(b, e, h):
                n = E * b + e
                for c in range(FC):
                    if positive(FC * (n - 1) + c + 1):
                        dve.wait_ge(v["z_lo"], FC * (n - 1) + c + 1)
                    dve.wait_ge(a["x2b"], FC * n + c + 1)
                    nc.vector.scalar_tensor_tensor(out=z[:, c, :], in0=bank[2 * c][:, :],
                                                   scalar=cols[:, bass.ds(FC * e + c, 1)],
                                                   in1=x2b[:, c, :], op0=ALU.add, op1=ALU.mult)\
                        .then_inc(v["z"], 1)
                for c in range(FC):
                    dve.wait_ge(a["z_hi"], FC * n + c + 1)
                    nc.vector.tensor_tensor(z_lo[:, h, c, :], z[:, c, :], z_hi[:, h, c, :].bitcast(F32),
                                            ALU.subtract).then_inc(v["z_lo"], 1)

            def accumulate(b, e):
                n = E * b + e
                dve.wait_ge(t["y"], n + 1)
                if positive(n):
                    dve.wait_ge(v["acc"], n)
                for c in range(C):
                    last = nc.vector.scalar_tensor_tensor(out=acc[:, b, c, :],
                                                          in0=bank[6][:, c * P:(c + 1) * P],
                                                          scalar=we[:, b, c, bass.ds(e, 1)],
                                                          in1=acc[:, b, c, :], op0=ALU.mult, op1=ALU.add)
                last.then_inc(v["acc"], 1)

            attention(0, 0)
            nc.vector.memset(w_pad[:], 0.0)
            nc.vector.memset(cwcb[:], 0.0)
            link(nc.vector.memset(mask_f[:], PAD))
            for stage in range(1, STAGES):
                attention(0, stage)
                if stage == 2:
                    dve.wait_ge(t["cols"], 1)
                    nc.vector.tensor_copy(cols[:], bank[7][:, 0:NROWS])
                    nc.vector.tensor_copy(ctxT[:], bank[7][:, NROWS:NROWS + B * T])
                    nc.vector.tensor_copy(WvT[:], bank[7][:, 256:384]).then_inc(v["cols"], 1)
                if stage == 3:
                    dve.wait_ge(t["WvWo"], 1)
                    nc.vector.tensor_copy(WvWo[:], bank[6][:, 0:P]).then_inc(v["WvWo"], 1)
                if stage == 5:
                    dve.wait_ge(v["cols"], 1)
                    nc.vector.tensor_copy(w_pad[:, QW - 1:QW], cols[:, WX:WX + 1])
                    dve.wait_ge(small_in, 16 * 3)
                    dve.wait_ge(t["txt"], 1)
                    nc.vector.tensor_copy(txtT[:], bank[7][:, 0:B * T])
                    full = (QT - 1) * Q4
                    for b in range(B):
                        for i in range(2):
                            at = (1 + i) * B * T + b * T
                            nc.vector.tensor_copy(
                                cwcb[:, i, b, :, 0:QT - 1],
                                bank[7][:, at:at + full].rearrange("p (i q) -> p q i", q=Q4))
                            nc.vector.tensor_copy(cwcb[:, i, b, 0, QT - 1:QT],
                                                  bank[7][:, at + full:at + T])
                        nc.vector.tensor_scalar(
                            mask_f[:, b, :, 0:QT - 1],
                            mask_i[:, b, 0:full].rearrange("p (i q) -> p q i", q=Q4),
                            -1.0, 1.0, ALU.mult, ALU.add)
                        last = nc.vector.tensor_scalar(mask_f[:, b, 0, QT - 1:QT], mask_i[:, b, full:T],
                                                       -1.0, 1.0, ALU.mult, ALU.add)
                    link(last)
                    for b in range(B):
                        nc.vector.tensor_scalar(mask_f[:, b, :, 0:QT - 1], mask_f[:, b, :, 0:QT - 1],
                                                NEG, None, ALU.mult)
                        nc.vector.tensor_scalar(mask_f[:, b, 0, QT - 1:QT], mask_f[:, b, 0, QT - 1:QT],
                                                NEG, None, ALU.mult)
                    dve.wait_ge(consts_ready, 2)
                    nc.vector.tensor_copy(expert_id[:], expert_i[:]).then_inc(v["txt"], 1)
                    dve.wait_ge(v["txt"], 1)
            attention(1, 0)
            dve.wait_ge(a["FT"], 1)
            add_group(0)
            add_group(1)
            for g in range(GROUPS):
                if g + 2 == GROUPS:
                    dve.wait_ge(a["FT"], 2)
                add_group(g + 2)
                attention(1, g + 1)
            for stage in range(4):
                cross_end(0, stage)
            glu(0, 0, 0)
            cross_end(0, 4)

            def between(place):
                for g in groups_at(place, -1):
                    add_group(g)
                for stage in stages_at.get(place, []):
                    cross_end(1, stage)

            cross_end(0, 5)
            for e in range(E):
                between(2 * e)
                glu(*following(0, e), (e + 1) % PAIR)
                if e == 0:
                    cross_end(0, 6)
                between(2 * e + 1)
                if e:
                    accumulate(0, e - 1)
            between(2 * E)
            glu(1, 1, 1)
            accumulate(0, E - 1)
            with dve.Fori(0, E // PAIR - 1) as pair:
                for h in range(PAIR):
                    glu(1, PAIR * pair + 2 + h, h)
                    accumulate(1, PAIR * pair + h)
            accumulate(1, E - 2)
            accumulate(1, E - 1)


_INS = ["x", "ctx_1024", "mask_BxS2_ik0", "L0_attn_Wq", "L0_attn_Wk", "L0_attn_Wv", "L0_attn_Wo",
        "L0_attn_bo", "L0_attn_gamma", "L0_attn_beta", "L0_xattn_Ws", "L0_xattn_W", "L0_xattn_w",
        "L0_xattn_b", "L0_xattn_Wcw", "L0_xattn_bcw", "L0_xattn_Wcb", "L0_xattn_bcb", "L0_ffn_gate_w",
        "L0_ffn_gate_b", "L0_ffn_w1", "L0_ffn_b1", "L0_ffn_w2", "L0_ffn_b2", "L0_ffn_wg", "L0_ffn_bg",
        "L0_ffn_w3", "L0_ffn_b3"]


def kernel(**inputs):
    import numpy as _np
    import concourse.bacc as _bacc
    from concourse import mybir as _mybir
    from concourse.bass_utils import run_bass_kernel_spmd as _run

    nc = _bacc.Bacc("TRN2", target_bir_lowering=False, num_devices=1)
    arrays, args = {}, []
    for name in _INS:
        a = _np.ascontiguousarray(inputs[name])
        arrays[f"in_{name}_dram"] = a
        args.append(nc.dram_tensor(f"in_{name}_dram", a.shape, _mybir.dt.from_np(a.dtype),
                                   kind="ExternalInput").ap())
    out = nc.dram_tensor("out_dram", inputs["x"].shape, _mybir.dt.float32, kind="ExternalOutput").ap()
    decoder_layer_program(nc, *args, out)
    r = _run(nc, [arrays], core_ids=[0])
    return r.results[0]["out_dram"]
```

```python
from contextlib import ExitStack

import concourse.bass as bass
from concourse import mybir

ALU = mybir.AluOpType
ACT = mybir.ActivationFunctionType
F32 = mybir.dt.float32
F32R = mybir.dt.float32r
I32 = mybir.dt.int32
U32 = mybir.dt.uint32
X = mybir.AxisListType.X

P = 128
EPS = 1e-5
NEG = -1e30
PAD = -3e38
ON_POOL = 3
PAIR = 2
STAGES = 10
RING = 4
AHEAD = RING - 1
GROUP = 8


def decoder_layer_program(nc, x, ctx, q_mask, Wq, Wk, Wv, Wo, bo, gamma, beta, Ws, W, w, xb, Wcw, bcw,
                          Wcb, bcb, gate_w, gate_b, w1, b1, w2, b2, wg, bg, w3, b3, out):
    B, L, D = x.shape
    T = ctx.shape[1]
    E, _, FF = w1.shape
    C = L // P
    FC = FF // P
    GROUPS = -(-T // GROUP)
    FIRST = T - (GROUPS - 1) * GROUP
    Q4 = 4
    QT = -(-T // Q4)
    QW = P // Q4
    TP = Q4 * QT
    assert D == P and L == C * P and 0 < FIRST <= GROUP and T % Q4 == 1 and QT <= QW
    LN = {}
    for kind in [(k, b) for b in range(B) for k in ("in", "attn", "x")] + [("ffn", b) for b in range(B)]:
        LN[kind] = len(LN)
    XB, WX, WCW, WCB = 3 * E * FC, 3 * E * FC + 1, 3 * E * FC + 2, 3 * E * FC + 3
    NROWS = 3 * E * FC + 4

    with ExitStack() as stack:
        def sb(name, shape, dt=F32):
            return stack.enter_context(nc.sbuf_tensor(name, shape, dt))

        def sem(name):
            return stack.enter_context(nc.semaphore(name))

        bank = [stack.enter_context(nc.psum_tensor(f"bank{i}", [P, 512], F32)) for i in range(8)]

        x_sb = sb("x_sb", [P, B * C, D])
        ctx_sb = sb("ctx_sb", [T, B, D])
        mask_i = sb("mask_i", [P, B, T], I32)
        wqkvo = sb("wqkvo", [P, 4, D])
        xw = sb("xw", [P, 2, D])
        rows = sb("rows", [NROWS, P])
        ln_rows = sb("ln_rows", [P, 3, D])
        small = sb("small", [P, E + 2])
        gate_sb = sb("gate_sb", [P, E])
        b3_sb = sb("b3_sb", [E, D])
        raw_w = sb("raw_w", [P, PAIR, (2 + FC) * FF])
        w_hi = sb("w_hi", [P, PAIR, (2 + FC) * FF], F32R)
        w_lo = sb("w_lo", [P, PAIR, (2 + FC) * FF], F32R)
        w3_sb = sb("w3_sb", [P, PAIR, FC, D])
        gate_hi = sb("gate_hi", [P, E], F32R)
        gate_lo = sb("gate_lo", [P, E], F32R)
        ident = sb("ident", [P, P])
        expert_i = sb("expert_i", [P, E], I32)
        expert_id = sb("expert_id", [P, E])
        minus_half = sb("minus_half", [P, C])
        cols = sb("cols", [P, NROWS])
        ctxT = sb("ctxT", [P, B * T])
        WvT = sb("WvT", [P, P])
        WvWo = sb("WvWo", [P, P])
        txtT = sb("txtT", [P, B * T])
        cwcb = sb("cwcb", [P, 2, B, Q4, QT])
        mask_f = sb("mask_f", [P, B, Q4, QT])
        w_pad = sb("w_pad", [P, 2 * QW - 1])
        stats = sb("stats", [P, C, 6])
        moments = sb("moments", [P, C, 2])
        var_eps = sb("var_eps", [P, C])
        rstd = sb("rstd", [P, C])
        h0 = sb("h0", [P, B, C, D])
        h0bo = sb("h0bo", [P, C, D])
        xbeta = sb("xbeta", [P, C, D])
        h0T = sb("h0T", [P, L])
        neg_qmax = sb("neg_qmax", [P, B, C])
        qsum = sb("qsum", [P, B, C])
        rq = sb("rq", [P, B, C])
        qE = sb("qE", [P, C, D])
        qET = sb("qET", [P, L])
        neg_kmax = sb("neg_kmax", [P, B])
        ksum = sb("ksum", [P, B])
        rk = sb("rk", [P, B])
        kET = sb("kET", [P, L])
        kE = sb("kE", [P, C, D])
        AT = sb("AT", [P, B, P])
        Cm = sb("Cm", [P, B, P])
        res = sb("res", [P, C, D])
        nrm = sb("nrm", [P, C, D])
        x1 = sb("x1", [P, B, C, D])
        h1 = sb("h1", [P, B, C, D])
        h1T = sb("h1T", [P, B, L])
        FT = sb("FT", [P, B, L])
        ring = sb("ring", [P, RING, GROUP, L])
        rhoT = sb("rhoT", [P, L])
        rho = sb("rho", [P, C, Q4, QT])
        rmax = sb("rmax", [P, C])
        att = sb("att", [P, 3, C, TP])
        sums = sb("sums", [P, 3, C])
        rden = sb("rden", [P, C])
        wsbs_pre = sb("wsbs_pre", [P, 2, C])
        wsbs = sb("wsbs", [P, 2, C])
        x2 = sb("x2", [P, C, D])
        h2 = sb("h2", [P, C, D])
        h2T_hi = sb("h2T_hi", [P, B, L], F32R)
        h2T_lo = sb("h2T_lo", [P, B, L], F32R)
        logits = sb("logits", [P, C, E])
        top = sb("top", [P, C, 8])
        top_i = sb("top_i", [P, C, 8], U32)
        top_f = sb("top_f", [P, C, 8])
        dtop = sb("dtop", [P, C])
        etop = sb("etop", [P, C])
        p1 = sb("p1", [P, C])
        p2 = sb("p2", [P, C])
        we1 = sb("we1", [P, C, E])
        we = sb("we", [P, B, C, E])
        weT = sb("weT", [E, L])
        x2b = sb("x2b", [P, FC, L])
        z = sb("z", [P, FC, L])
        z_hi = sb("z_hi", [P, 2, FC, L], F32R)
        z_lo = sb("z_lo", [P, 2, FC, L], F32R)
        s = sb("s", [P, FC, L])
        acc = sb("acc", [P, B, C, D])

        x_in = [sem(f"x_in{b}") for b in range(B)]
        mask_in, attn_w_in, ctx_in, rows_in, ln_rows_in, xw_in, small_in, gate_in = (
            sem(n) for n in ("mask_in", "attn_w_in", "ctx_in", "rows_in", "ln_rows_in", "xw_in", "small_in",
                             "gate_in"))
        up_w_in = [sem(f"up_w_in{h}") for h in range(PAIR)]
        gate_w_in = [sem(f"gate_w_in{h}") for h in range(PAIR)]
        w3_in = [sem(f"w3_in{h}") for h in range(PAIR)]
        pool_hi, up_split, wg_split, router_split, pool_added = (
            sem(n) for n in ("pool_hi", "up_split", "wg_split", "router_split", "pool_added"))
        out_stored = sem("out_stored")
        zeroed, ident_ready, consts_ready, rstd_ready, pool_rows = (
            sem(n) for n in ("zeroed", "ident_ready", "consts_ready", "rstd_ready", "pool_rows"))
        chain = sem("vector_chain")
        var_ready = sem("var_ready")
        v = {n: sem("v_" + n) for n in (
            "cols", "WvT", "WvWo", "txt", "h0", "neg_kmax", "neg_qmax", "kE", "AT", "C", "h1", "added",
            "centred", "exp_in", "wsbs_pre", "h2", "h2T_lo", "dtop", "we", "weT", "z", "z_lo", "acc",
            "acc_start", "acc_last")}
        copied = {n: sem("copied_" + n) for n in ("h0T", "qET", "h1T", "FT")}
        a = {n: sem("a_" + n) for n in (
            "kexp", "qexp", "rhoT", "tanh", "att", "wsbs", "h2T", "etop", "x2b", "z_hi", "silu")}
        t = {n: sem("t_" + n) for n in (
            "cols", "WvWo", "txt", "h0T", "q", "k", "kE", "qET", "AT", "C", "out", "h1T", "FT", "rhoT",
            "rho", "h2T", "gate", "weT", "b3", "x12", "g", "y", "y_last")}

        block = stack.enter_context(nc.Block())

        def text_group(g):
            b, k = divmod(g, GROUPS)
            return b, FIRST + (k - 1) * GROUP if k else 0, GROUP if k else FIRST, g % RING

        second_on_pool = {0: FIRST, 1: 5, 2: 5, 3: 5, 4: GROUP, 5: GROUP}

        def on_pool(g):
            if g == 0:
                return FIRST // 2
            return ON_POOL if g < GROUPS else second_on_pool.get(g - GROUPS, 0)

        def pool_groups(g):
            return sum(1 for k in range(g + 1) if on_pool(k))

        def vector_groups(g):
            return sum(1 for k in range(g + 1) if on_pool(k) < text_group(k)[2])

        LATE = GROUPS + 5
        tanh_place = {g: g - LATE + (2 if g > LATE else 1) for g in range(LATE, B * GROUPS)}

        def groups_at(place):
            return [g for g in tanh_place if tanh_place[g] == place]

        END = tanh_place[B * GROUPS - 1] + 2
        stages_at = {END: [0], END + 1: [1], END + 2: [2], END + 3: [3, 4], END + 4: [5], END + 5: [6],
                     END + 6: [7], END + 7: [8], END + 8: [9]}
        assert END + 8 <= 2 * E

        attention_at = [[1], [2], [3, 4], [5], [6], [7], [], [8], [9], []]

        def positive(value):
            return not (isinstance(value, int) and value <= 0)

        attention_banks = [bank[0:4], bank[4:7] + [bank[3]]]
        end_bank = [bank[6], bank[7]]

        def following(b, e):
            return (b, e + 1) if e + 1 < E else (b + 1, 0)

        @block.sync
        def _(sp):
            def load_x(b):
                sp.dma_start(x_sb[:, b * C:(b + 1) * C, :],
                             x[b].rearrange("(c p) d -> p c d", p=P)).then_inc(x_in[b], 16)

            load_x(0)
            sp.dma_start(rows[XB:XB + 1, :], xb).then_inc(rows_in, 16)
            sp.dma_start(rows[WX:WX + 1, :], w.rearrange("d o -> o d")).then_inc(rows_in, 16)
            sp.dma_start(rows[WCW:WCW + 1, :], Wcw).then_inc(rows_in, 16)
            sp.dma_start(rows[WCB:WCB + 1, :], Wcb).then_inc(rows_in, 16)
            for i, m in enumerate((b1, b2, bg)):
                sp.dma_start(rows[i * E * FC:(i + 1) * E * FC, :], m.rearrange("e (c p) -> (e c) p", p=P))\
                    .then_inc(rows_in, 16)
            sp.dma_start(ctx_sb[:], ctx.rearrange("b t d -> t b d")).then_inc(ctx_in, 16)
            for i, m in enumerate((bo, gamma, beta)):
                sp.dma_start(ln_rows[:, i, :], m.rearrange("(o d) -> o d", o=1).broadcast_to([P, D]))\
                    .then_inc(ln_rows_in, 16)
            for i, m in enumerate((Ws, W)):
                sp.dma_start(xw[:, i, :], m).then_inc(xw_in, 16)
            for b in range(1, B):
                load_x(b)

            def load_up(e, h):
                sp.dma_start(raw_w[:, h, 0:FF], w1[e]).then_inc(up_w_in[h], 16)
                sp.dma_start(raw_w[:, h, FF:2 * FF], w2[e]).then_inc(up_w_in[h], 16)

            def load_gate(e, h):
                sp.dma_start(raw_w[:, h, 2 * FF:].rearrange("p (k f) -> p k f", k=FC),
                             wg[e].rearrange("(k p) f -> p k f", p=P)).then_inc(gate_w_in[h], 16)

            def load_down(e, h):
                sp.dma_start(w3_sb[:, h, :, :], w3[e].rearrange("(k p) f -> p k f", p=P))\
                    .then_inc(w3_in[h], 16)

            def load_step(n, e, e_before, h):
                sp.wait_ge(up_split, n - 1)
                load_up(e, h)
                sp.wait_ge(wg_split, n - 1)
                load_gate(e, h)
                if positive(n - 2):
                    sp.wait_ge(t["y"], n - 2)
                load_down(e_before, 1 - h)

            for h in range(PAIR):
                load_up(h, h)
                load_gate(h, h)
            load_down(0, 0)
            for b in range(B):
                peeled = PAIR if b == 0 else 0
                for e in range(peeled, peeled + PAIR):
                    load_step(E * b + e, e, (e - 1) % E, e % PAIR)
                with sp.Fori(peeled // PAIR + 1, E // PAIR) as pair:
                    for h in range(PAIR):
                        e = PAIR * pair + h
                        load_step(E * b + e, e, PAIR * pair + h - 1, h)
            sp.wait_ge(t["y"], B * E - 2)
            load_down(E - 1, (B * E - 1) % PAIR)
            for b in range(B - 1):
                sp.wait_ge(v["acc"], E * (b + 1))
                sp.dma_start(out[b].rearrange("(c p) d -> p c d", p=P), acc[:, b, :, :])\
                    .then_inc(out_stored, 16)
            half = C // 2
            for c in range(0, C, half):
                sp.wait_ge(v["acc_last"], c + half)
                sp.dma_start(out[B - 1, c * P:(c + half) * P].rearrange("(c p) d -> p c d", p=P),
                             acc[:, B - 1, c:c + half, :]).then_inc(out_stored, 16)
            sp.wait_ge(out_stored, 16 * (B - 1 + C // half))

        @block.gpsimd
        def _(pool):
            nc.gpsimd.memset(ident[:], 0.0).then_inc(zeroed, 1)
            nc.gpsimd.memset(minus_half[:], -0.5).then_inc(consts_ready, 1)
            nc.gpsimd.iota(expert_i[:], pattern=[[1, E]], base=0, channel_multiplier=0)\
                .then_inc(consts_ready, 1)
            pool.wait_ge(zeroed, 1)
            nc.gpsimd.affine_select(out=ident[:], in_=ident[:], compare_op=ALU.not_equal, fill=1.0, base=0,
                                    pattern=[[-1, P]], channel_multiplier=1).then_inc(ident_ready, 1)
            pool.wait_ge(consts_ready, 2)

            def add_group(g):
                b, t0, n, slot = text_group(g)
                if g >= RING:
                    pool.wait_ge(t["rho"], g - RING + 1)
                for i in range(n - on_pool(g), n):
                    last = nc.gpsimd.tensor_scalar(ring[:, slot, i, :], FT[:, b, :],
                                                   txtT[:, b * T + t0 + i:b * T + t0 + i + 1], 1.0,
                                                   ALU.add, ALU.mult)
                last.then_inc(pool_added, 1)

            def rstd_of():
                nonlocal ln
                pool.wait_ge(var_ready, ln + 1)
                nc.gpsimd.tensor_tensor(rstd[:], var_eps[:], minus_half[:], ALU.pow)\
                    .then_inc(rstd_ready, 1)
                ln += 1

            def attention_rows(b):
                pool.wait_ge(ln_rows_in, 16 * 3)
                pool.wait_ge(v["h0"], b + 1)
                nc.gpsimd.tensor_tensor(h0bo[:], h0[:, b],
                                        ln_rows[:, 0:1, :].broadcast_to([P, C, D]), ALU.add)\
                    .then_inc(pool_rows, 1)
                nc.gpsimd.tensor_tensor(xbeta[:], x_sb[:, b * C:(b + 1) * C, :],
                                        ln_rows[:, 2:3, :].broadcast_to([P, C, D]), ALU.add)\
                    .then_inc(pool_rows, 1)

            splits = 0

            def split(hi, lo, src, done):
                nonlocal splits
                splits += 1
                nc.gpsimd.tensor_scalar(hi, src, 0.0, 1.0, ALU.add, ALU.mult).then_inc(pool_hi, 1)
                pool.wait_ge(pool_hi, splits)
                nc.gpsimd.tensor_tensor(lo, src, hi.bitcast(F32), ALU.subtract).then_inc(done, 1)

            def split_up(n):
                h = n % PAIR
                pool.wait_ge(up_w_in[h], 32 * (n // PAIR + 1))
                if positive(n - 1):
                    pool.wait_ge(t["x12"], FC * (n - 1))
                split(w_hi[:, h, 0:2 * FF], w_lo[:, h, 0:2 * FF], raw_w[:, h, 0:2 * FF], up_split)

            def split_wg(n):
                h = n % PAIR
                pool.wait_ge(gate_w_in[h], 16 * (n // PAIR + 1))
                if positive(n - 1):
                    pool.wait_ge(t["g"], FC * (n - 1))
                split(w_hi[:, h, 2 * FF:], w_lo[:, h, 2 * FF:], raw_w[:, h, 2 * FF:], wg_split)

            ln = 0
            nc.gpsimd.dma_start(mask_i[:], q_mask.rearrange("(o b) t -> o b t", o=1)
                                .broadcast_to([P, B, T])).then_inc(mask_in, 16)
            rstd_of()
            attention_rows(0)
            nc.gpsimd.dma_start(small[:, E:E + 1], bcw.rearrange("(o e) -> o e", o=1).broadcast_to([P, 1]))\
                .then_inc(small_in, 16)
            nc.gpsimd.dma_start(small[:, E + 1:E + 2], bcb.rearrange("(o e) -> o e", o=1)
                                .broadcast_to([P, 1])).then_inc(small_in, 16)
            nc.gpsimd.dma_start(gate_sb[:], gate_w).then_inc(gate_in, 16)
            nc.gpsimd.dma_start(small[:, 0:E], gate_b.rearrange("(o e) -> o e", o=1).broadcast_to([P, E]))\
                .then_inc(gate_in, 16)
            nc.gpsimd.dma_start(b3_sb[:], b3).then_inc(gate_in, 16)
            rstd_of()
            rstd_of()
            rstd_of()
            pool.wait_ge(copied["FT"], 1)
            pool.wait_ge(v["txt"], 1)
            for g in range(AHEAD):
                add_group(g)
            attention_rows(1)
            for g in range(GROUPS):
                if g + AHEAD < GROUPS:
                    add_group(g + AHEAD)
                if g == 0:
                    pool.wait_ge(gate_in, 48)
                    split(gate_hi[:], gate_lo[:], gate_sb[:], router_split)
                if g == 1:
                    split_up(0)
                if g == 2:
                    split_wg(0)
                if g == 3:
                    split_up(1)
                for _ in {5, 7} & set(attention_at[g]):
                    rstd_of()
            pool.wait_ge(copied["FT"], 2)
            add_group(GROUPS)
            add_group(GROUPS + 1)
            add_group(GROUPS + 2)
            rstd_of()
            add_group(GROUPS + 3)
            add_group(GROUPS + 4)
            for n in range(1, B * E):
                if n == (END + 3) // 2 + 2:
                    rstd_of()
                split_wg(n)
                if n == 1:
                    add_group(LATE)
                if n + 1 < B * E:
                    split_up(n + 1)

        @block.scalar
        def _(act):
            for i in (1, 0, 2, 3):
                act.dma_start(wqkvo[:, i, :], (Wq, Wk, Wv, Wo)[i]).then_inc(attn_w_in, 16)

            def attention(b, stage):
                A, Q, K, M = attention_banks[b]
                if stage == 1 and b == 0:
                    act.wait_ge(t["h0T"], b + 1)
                    nc.scalar.copy(h0T[:, :], A[:, :]).then_inc(copied["h0T"], 1)
                if stage == 2:
                    act.wait_ge(t["k"], b + 1)
                    act.wait_ge(v["neg_kmax"], b + 1)
                    nc.scalar.activation(kET[:, :], K[:, :], ACT.Exp, bias=neg_kmax[:, b:b + 1],
                                         accum_out=ksum[:, b:b + 1]).then_inc(a["kexp"], 1)
                    act.wait_ge(v["neg_qmax"], b + 1)
                    for c in range(C):
                        nc.scalar.activation(qE[:, c, :], Q[:, c * P:(c + 1) * P], ACT.Exp,
                                             bias=neg_qmax[:, b, c:c + 1],
                                             accum_out=qsum[:, b, c:c + 1]).then_inc(a["qexp"], 1)
                if stage == 3 and b == 0:
                    act.wait_ge(t["qET"], b + 1)
                    nc.scalar.copy(qET[:, :], Q[:, :]).then_inc(copied["qET"], 1)
                if stage == 8 and b == 0:
                    act.wait_ge(t["h1T"], b + 1)
                    nc.scalar.copy(h1T[:, b, :], M[:, :]).then_inc(copied["h1T"], 1)
                if stage == 9 and b == 0:
                    act.wait_ge(t["FT"], b + 1)
                    act.wait_ge(v["cols"], 1)
                    act.wait_ge(small_in, 16 * 2)
                    nc.scalar.activation(FT[:, b, :], A[:, :], ACT.Identity, bias=cols[:, XB:XB + 1])\
                        .then_inc(copied["FT"], 1)

            def tanh_group(g):
                _, _, n, slot = text_group(g)
                if on_pool(g) < n:
                    act.wait_ge(v["added"], vector_groups(g))
                if on_pool(g):
                    act.wait_ge(pool_added, pool_groups(g))
                nc.scalar.activation(ring[:, slot, 0:n, :], ring[:, slot, 0:n, :], ACT.Tanh)\
                    .then_inc(a["tanh"], 1)

            def cross_end(b, stage):
                if stage == 0:
                    act.wait_ge(t["rho"], GROUPS * (b + 1))
                    nc.scalar.copy(rhoT[:], bank[7][:, :]).then_inc(a["rhoT"], 1)
                if stage == 1:
                    act.wait_ge(v["exp_in"], b + 1)
                    nc.scalar.activation(att[:, 0, :, :], rho[:].rearrange("p c q i -> p c (q i)"),
                                         ACT.Exp).then_inc(a["att"], 1)
                if stage == 3:
                    act.wait_ge(v["wsbs_pre"], b + 1)
                    nc.scalar.activation(wsbs[:, 0, :], wsbs_pre[:, 0, :], ACT.Tanh, bias=small[:, E:E + 1])
                    nc.scalar.activation(wsbs[:, 1, :], wsbs_pre[:, 1, :], ACT.Tanh,
                                         bias=small[:, E + 1:E + 2]).then_inc(a["wsbs"], 1)
                if stage == 6:
                    act.wait_ge(t["h2T"], b + 1)
                    nc.scalar.copy(h2T_hi[:, b, :], end_bank[b][:, :]).then_inc(a["h2T"], 1)
                if stage == 7:
                    act.wait_ge(v["dtop"], b + 1)
                    nc.scalar.activation(etop[:], dtop[:], ACT.Exp).then_inc(a["etop"], 1)

            def glu_part(b, e, h):
                n = E * b + e
                for c in range(FC):
                    act.wait_ge(t["x12"], FC * n + c + 1)
                    if positive(FC * (n - 1) + c + 1):
                        act.wait_ge(v["z"], FC * (n - 1) + c + 1)
                    nc.scalar.activation(x2b[:, c, :], bank[2 * c + 1][:, :], ACT.Identity,
                                         bias=cols[:, bass.ds(E * FC + FC * e + c, 1)]).then_inc(a["x2b"], 1)
                for c in range(FC):
                    act.wait_ge(v["z"], FC * n + c + 1)
                    if positive(n - 1):
                        act.wait_ge(t["g"], FC * (n - 1))
                    nc.scalar.copy(z_hi[:, h, c, :], z[:, c, :]).then_inc(a["z_hi"], 1)

            def silu_part(b, e):
                n = E * b + e
                for c in range(FC):
                    act.wait_ge(t["g"], FC * n + c + 1)
                    nc.scalar.activation(s[:, c, :], bank[4 + c][:, :], ACT.Silu,
                                         bias=cols[:, bass.ds(2 * E * FC + FC * e + c, 1)])\
                        .then_inc(a["silu"], 1)

            for stage in range(STAGES):
                attention(0, stage)
            tanh_group(0)
            for g in range(GROUPS):
                if g + 1 < GROUPS:
                    tanh_group(g + 1)
                for stage in attention_at[g]:
                    attention(1, stage)
            cross_end(0, 0)
            cross_end(0, 1)
            tanh_group(GROUPS)
            cross_end(0, 3)
            tanh_group(GROUPS + 1)
            tanh_group(GROUPS + 2)
            cross_end(0, 6)
            tanh_group(GROUPS + 3)
            glu_part(0, 0, 0)
            tanh_group(GROUPS + 4)
            cross_end(0, 7)

            def between(place):
                for g in groups_at(place):
                    tanh_group(g)
                for stage in stages_at.get(place, []):
                    cross_end(1, stage)

            for e in range(E):
                between(2 * e)
                glu_part(*following(0, e), (e + 1) % PAIR)
                between(2 * e + 1)
                silu_part(0, e)
            glu_part(1, 1, 1)
            silu_part(1, 0)
            with act.Fori(0, E // PAIR - 1) as pair:
                for h in range(PAIR):
                    glu_part(1, PAIR * pair + 2 + h, h)
                    silu_part(1, PAIR * pair + 1 + h)
            silu_part(1, E - 1)

        @block.tensor
        def _(pe):
            def transposed(out_ap, in_ap, k):
                return nc.tensor.transpose(out_ap, in_ap, ident[0:k, 0:k])

            def exact_product(acc_ap, operands):
                parts = [x for l_hi, l_lo, r_hi, r_lo in operands
                         for x in ((l_hi, r_hi), (l_hi, r_lo), (l_lo, r_hi))]
                for i, (lhsT, rhs) in enumerate(parts):
                    mm = nc.tensor.matmul(acc_ap, lhsT, rhs, start=(i == 0), stop=(i == len(parts) - 1))
                return mm

            def attention(b, stage):
                A, Q, K, M = attention_banks[b]
                if stage == 1:
                    pe.wait_ge(v["h0"], b + 1)
                    for c in range(C):
                        mm = transposed(A[:, c * P:(c + 1) * P], h0[:, b, c, :], P)
                    mm.then_inc(t["h0T"], 1)
                    pe.wait_ge(copied["h0T"], b + 1)
                    nc.tensor.matmul(K[:, :], wqkvo[:, 1, :], h0T[:, :], start=True, stop=True)\
                        .then_inc(t["k"], 1)
                    for c in range(C):
                        mm = nc.tensor.matmul(Q[:, c * P:(c + 1) * P], h0T[:, c * P:(c + 1) * P],
                                              wqkvo[:, 0, :], start=True, stop=True)
                    mm.then_inc(t["q"], 1)
                if stage == 3:
                    pe.wait_ge(a["kexp"], b + 1)
                    for c in range(C):
                        mm = transposed(A[:, c * P:(c + 1) * P], kET[:, c * P:(c + 1) * P], P)
                    mm.then_inc(t["kE"], 1)
                    pe.wait_ge(a["qexp"], C * (b + 1))
                    for c in range(C):
                        mm = transposed(Q[:, c * P:(c + 1) * P], qE[:, c, :], P)
                    mm.then_inc(t["qET"], 1)
                if stage == 4:
                    pe.wait_ge(v["kE"], b + 1)
                    for c in range(C):
                        mm = nc.tensor.matmul(K[:, 0:P], h0[:, b, c, :], kE[:, c, :],
                                              start=(c == 0), stop=(c == C - 1))
                    mm.then_inc(t["AT"], 1)
                    pe.wait_ge(v["AT"], b + 1)
                    nc.tensor.matmul(K[:, P:2 * P], AT[:, b, :], WvWo[:], start=True, stop=True)\
                        .then_inc(t["C"], 1)
                if stage == 5:
                    pe.wait_ge(copied["qET"], b + 1)
                    pe.wait_ge(v["C"], b + 1)
                    for c in range(C):
                        mm = nc.tensor.matmul(A[:, c * P:(c + 1) * P], qET[:, c * P:(c + 1) * P],
                                              Cm[:, b, :], start=True, stop=True)
                    mm.then_inc(t["out"], 1)
                if stage == 8:
                    pe.wait_ge(v["h1"], b + 1)
                    for c in range(C):
                        mm = transposed(M[:, c * P:(c + 1) * P], h1[:, b, c, :], P)
                    mm.then_inc(t["h1T"], 1)
                if stage == 9:
                    pe.wait_ge(copied["h1T"], b + 1)
                    nc.tensor.matmul(A[:, :], xw[:, 1, :], h1T[:, b, :], start=True, stop=True)\
                        .then_inc(t["FT"], 1)

            def score_group(g):
                b, t0, n, slot = text_group(g)
                pe.wait_ge(a["tanh"], g + 1)
                if b and t0 == 0:
                    pe.wait_ge(a["rhoT"], b)
                for i in range(n):
                    q, row = (t0 + i) % Q4, (t0 + i) // Q4
                    mm = nc.tensor.matmul(bank[7][q * QW:(q + 1) * QW, :],
                                          w_pad[:, QW - 1 - row:2 * QW - 1 - row],
                                          ring[:, slot, i, :], start=(row == 0),
                                          stop=(t0 + i + Q4 >= T))
                mm.then_inc(t["rho"], 1)

            def cross_end(b, stage):
                R = end_bank[b]
                if stage == 0:
                    pe.wait_ge(a["rhoT"], b + 1)
                    for c in range(C):
                        mm = transposed(R[:, c * P:(c + 1) * P], rhoT[:, c * P:(c + 1) * P], P)
                    mm.then_inc(t["rhoT"], 1)
                if stage == 6:
                    pe.wait_ge(v["h2"], b + 1)
                    for c in range(C):
                        mm = transposed(R[:, c * P:(c + 1) * P], h2[:, c, :], P)
                    mm.then_inc(t["h2T"], 1)
                if stage == 7:
                    pe.wait_ge(a["h2T"], b + 1)
                    pe.wait_ge(v["h2T_lo"], b + 1)
                    pe.wait_ge(router_split, 1)
                    for c in range(C):
                        col = slice(c * P, (c + 1) * P)
                        mm = exact_product(R[:, c * E:(c + 1) * E],
                                           [(h2T_hi[:, b, col], h2T_lo[:, b, col], gate_hi[:], gate_lo[:])])
                    mm.then_inc(t["gate"], 1)
                if stage == 8:
                    pe.wait_ge(v["we"], b + 1)
                    for c in range(C):
                        mm = transposed(R[0:E, c * P:(c + 1) * P], we[:, b, c, :], P)
                    mm.then_inc(t["weT"], 1)
                if stage == 9:
                    pe.wait_ge(v["weT"], b + 1)
                    for c in range(C):
                        mm = nc.tensor.matmul(R[:, c * P:(c + 1) * P], weT[:, c * P:(c + 1) * P],
                                              b3_sb[:], start=True, stop=True)
                    mm.then_inc(t["b3"], 1)

            def expert_up(b, e, h):
                n = E * b + e
                pe.wait_ge(up_split, n + 1)
                if not positive(e):
                    pe.wait_ge(a["h2T"], b + 1)
                    pe.wait_ge(v["h2T_lo"], b + 1)
                for c in range(FC):
                    if positive(FC * (n - 1) + c + 1):
                        pe.wait_ge(v["z"], FC * (n - 1) + c + 1)
                    for i in range(2):
                        col = slice(i * FF + c * P, i * FF + (c + 1) * P)
                        mm = exact_product(bank[2 * c + i][:, :], [(w_hi[:, h, col], w_lo[:, h, col],
                                                                    h2T_hi[:, b, :], h2T_lo[:, b, :])])
                    mm.then_inc(t["x12"], 1)

            def expert_gate(b, e, h):
                n = E * b + e
                for c in range(FC):
                    if positive(FC * (n - 1) + c + 1):
                        pe.wait_ge(a["silu"], FC * (n - 1) + c + 1)
                    if c == 0:
                        pe.wait_ge(wg_split, n + 1)
                        pe.wait_ge(v["z_lo"], FC * n + FC)
                    cols_of = [slice((2 + k) * FF + c * P, (2 + k) * FF + (c + 1) * P) for k in range(FC)]
                    exact_product(bank[4 + c][:, :], [(w_hi[:, h, col], w_lo[:, h, col],
                                                       z_hi[:, h, k, :], z_lo[:, h, k, :])
                                                      for k, col in enumerate(cols_of)])\
                        .then_inc(t["g"], 1)

            def expert_down(b, e, h, turn):
                n = E * b + e
                pe.wait_ge(w3_in[h], 16 * (turn + 1))
                pe.wait_ge(a["silu"], FC * n + FC)
                if positive(n):
                    pe.wait_ge(v["acc"], n)
                else:
                    pe.wait_ge(v["acc_start"], 1)
                for c in range(C):
                    for k in range(FC):
                        mm = nc.tensor.matmul(bank[6][:, c * P:(c + 1) * P], s[:, k, c * P:(c + 1) * P],
                                              w3_sb[:, h, k, :], start=(k == 0), stop=(k == FC - 1))
                mm.then_inc(t["y"], 1)

            def last_down():
                h = (B * E - 1) % PAIR
                pe.wait_ge(w3_in[h], 16 * (B * E // PAIR))
                pe.wait_ge(a["silu"], FC * B * E)
                for c in range(C):
                    for k in range(FC):
                        mm = nc.tensor.matmul(bank[c][:, 0:P], s[:, k, c * P:(c + 1) * P],
                                              w3_sb[:, h, k, :], start=(k == 0), stop=(k == FC - 1))
                    mm.then_inc(t["y_last"], 1)

            def keep_clock(n):
                for _ in range(n):
                    transposed(bank[5][:, 0:P], ident[:], P)

            pe.wait_ge(ident_ready, 1)
            keep_clock(28)
            pe.wait_ge(attn_w_in, 64)
            attention(0, 1)
            transposed(bank[7][:, 256:384], wqkvo[:, 2, :], P)
            pe.wait_ge(rows_in, 16 * 7)
            transposed(bank[7][:, 0:NROWS], rows[:], NROWS)
            pe.wait_ge(ctx_in, 16)
            for b in range(B):
                mm = transposed(bank[7][:, NROWS + b * T:NROWS + (b + 1) * T], ctx_sb[:, b, :], T)
            mm.then_inc(t["cols"], 1)
            attention(0, 3)
            pe.wait_ge(v["cols"], 1)
            nc.tensor.matmul(bank[6][:, 0:P], WvT[:], wqkvo[:, 3, :], start=True, stop=True)\
                .then_inc(t["WvWo"], 1)
            pe.wait_ge(v["WvWo"], 1)
            attention(0, 4)
            attention(0, 5)
            pe.wait_ge(xw_in, 32)
            nc.tensor.matmul(bank[7][:, 0:B * T], xw[:, 0, :], ctxT[:], start=True, stop=True)
            for i, col in enumerate((WCW, WCB)):
                mm = nc.tensor.matmul(bank[7][:, (1 + i) * B * T:(2 + i) * B * T],
                                      cols[:, col:col + 1].broadcast_to([P, P]), ctxT[:],
                                      start=True, stop=True)
            mm.then_inc(t["txt"], 1)
            keep_clock(66)
            attention(0, 8)
            keep_clock(6)
            attention(0, 9)
            keep_clock(36)
            pe.wait_ge(v["txt"], 1)
            for g in range(GROUPS):
                score_group(g)
                for stage in attention_at[g]:
                    attention(1, stage)
            cross_end(0, 0)
            keep_clock(36)
            score_group(GROUPS)
            keep_clock(20)
            score_group(GROUPS + 1)
            cross_end(0, 6)
            score_group(GROUPS + 2)
            expert_up(0, 0, 0)
            cross_end(0, 7)
            score_group(GROUPS + 3)

            def between(place):
                for g in groups_at(place - 2):
                    score_group(g)
                for stage in stages_at.get(place, []):
                    cross_end(1, stage)

            for e in range(E):
                between(2 * e)
                expert_up(*following(0, e), (e + 1) % PAIR)
                if e:
                    expert_down(0, e - 1, (e - 1) % PAIR, (e - 1) // PAIR)
                between(2 * e + 1)
                expert_gate(0, e, e % PAIR)
                if e == 0:
                    cross_end(0, 8)
                    score_group(GROUPS + 4)
                    cross_end(0, 9)
            between(2 * E)
            expert_up(1, 1, 1)
            expert_down(0, E - 1, 1, E // PAIR - 1)
            expert_gate(1, 0, 0)
            with pe.Fori(0, E // PAIR - 1) as pair:
                for h in range(PAIR):
                    expert_up(1, PAIR * pair + 2 + h, h)
                    expert_down(1, PAIR * pair + h, h, pair + E // PAIR)
                    expert_gate(1, PAIR * pair + 1 + h, 1 - h)
            expert_down(1, E - 2, 0, B * E // PAIR - 1)
            expert_gate(1, E - 1, 1)
            last_down()

        @block.vector
        def _(dve):
            links = 0

            def link(ins):
                nonlocal links
                links += 1
                ins.then_inc(chain, 1)
                dve.wait_ge(chain, links)

            def norm_stats(src):
                for c in range(C):
                    last = nc.vector.bn_stats(stats[:, c, :], src[:, c, :])
                link(last)
                for c in range(C):
                    last = nc.vector.bn_aggr(moments[:, c, :], stats[:, c, :])
                link(last)
                nc.vector.tensor_scalar(var_eps[:], moments[:, :, 1], EPS, None, ALU.add)\
                    .then_inc(var_ready, 1)

            def norm_apply(which, src, dst):
                dve.wait_ge(rstd_ready, LN[which] + 1)
                for c in range(C):
                    last = nc.vector.tensor_scalar(dst[:, c, :], src[:, c, :], moments[:, c, 0:1],
                                                   rstd[:, c:c + 1], ALU.subtract, ALU.mult)
                return last

            def attention(b, stage):
                A, Q, K, M = attention_banks[b]
                xs = x_sb[:, b * C:(b + 1) * C]
                if stage == 0:
                    dve.wait_ge(x_in[b], 16)
                    norm_stats(xs)
                    norm_apply(("in", b), xs, h0[:, b]).then_inc(v["h0"], 1)
                if stage == 1 and b > 0:
                    dve.wait_ge(t["h0T"], b + 1)
                    nc.vector.tensor_copy(h0T[:, :], A[:, :]).then_inc(copied["h0T"], 1)
                if stage == 2:
                    dve.wait_ge(t["k"], b + 1)
                    nc.vector.tensor_reduce(neg_kmax[:, b:b + 1], K[:, :], X, ALU.max, negate=True)\
                        .then_inc(v["neg_kmax"], 1)
                    dve.wait_ge(t["q"], b + 1)
                    nc.vector.tensor_reduce(neg_qmax[:, b, :], Q[:, :].rearrange("p (c d) -> p c d", c=C),
                                            X, ALU.max, negate=True).then_inc(v["neg_qmax"], 1)
                if stage == 3:
                    dve.wait_ge(t["kE"], b + 1)
                    nc.vector.tensor_copy(kE[:].rearrange("p c d -> p (c d)"), A[:, :])\
                        .then_inc(v["kE"], 1)
                    if b > 0:
                        dve.wait_ge(t["qET"], b + 1)
                        nc.vector.tensor_copy(qET[:, :], Q[:, :]).then_inc(copied["qET"], 1)
                if stage == 4:
                    dve.wait_ge(a["kexp"], b + 1)
                    nc.vector.reciprocal(rk[:, b:b + 1], ksum[:, b:b + 1])
                    dve.wait_ge(a["qexp"], C * (b + 1))
                    link(nc.vector.reciprocal(rq[:, b, :], qsum[:, b, :]))
                    dve.wait_ge(t["AT"], b + 1)
                    nc.vector.tensor_copy(AT[:, b, :], K[:, 0:P]).then_inc(v["AT"], 1)
                    dve.wait_ge(t["C"], b + 1)
                    nc.vector.tensor_scalar(Cm[:, b, :], K[:, P:2 * P], rk[:, b:b + 1], float(D) ** -0.5,
                                            ALU.mult, ALU.mult).then_inc(v["C"], 1)
                if stage == 5:
                    dve.wait_ge(t["out"], b + 1)
                    dve.wait_ge(pool_rows, 2 * (b + 1))
                    for c in range(C):
                        last = nc.vector.scalar_tensor_tensor(
                            out=res[:, c, :], in0=A[:, c * P:(c + 1) * P], scalar=rq[:, b, c:c + 1],
                            in1=h0bo[:, c, :], op0=ALU.mult, op1=ALU.add)
                    link(last)
                    norm_stats(res[:])
                    for c in range(C):
                        last = nc.vector.scalar_tensor_tensor(
                            out=nrm[:, c, :], in0=res[:, c, :], scalar=moments[:, c, 0:1],
                            in1=ln_rows[:, 1, :], op0=ALU.subtract, op1=ALU.mult)
                    last.then_inc(v["centred"], 1)
                if stage == 6:
                    dve.wait_ge(v["centred"], b + 1)
                    dve.wait_ge(rstd_ready, LN[("attn", b)] + 1)
                    for c in range(C):
                        last = nc.vector.scalar_tensor_tensor(
                            out=x1[:, b, c, :], in0=nrm[:, c, :], scalar=rstd[:, c:c + 1],
                            in1=xbeta[:, c, :], op0=ALU.mult, op1=ALU.add)
                    link(last)
                if stage == 7:
                    norm_stats(x1[:, b])
                if stage == 8:
                    norm_apply(("x", b), x1[:, b], h1[:, b]).then_inc(v["h1"], 1)
                    if b > 0:
                        dve.wait_ge(t["h1T"], b + 1)
                        nc.vector.tensor_copy(h1T[:, b, :], M[:, :]).then_inc(copied["h1T"], 1)
                if stage == 9:
                    if b > 0:
                        dve.wait_ge(t["FT"], b + 1)
                        nc.vector.tensor_scalar(FT[:, b, :], A[:, :], cols[:, XB:XB + 1], None,
                                                ALU.add).then_inc(copied["FT"], 1)

            def add_group(g):
                b, t0, n, slot = text_group(g)
                if g >= RING:
                    dve.wait_ge(t["rho"], g - RING + 1)
                for i in range(n - on_pool(g)):
                    last = nc.vector.tensor_scalar(ring[:, slot, i, :], FT[:, b, :],
                                                   txtT[:, b * T + t0 + i:b * T + t0 + i + 1], None, ALU.add)
                last.then_inc(v["added"], 1)

            def cross_end(b, stage):
                R = end_bank[b]
                if stage == 0:
                    dve.wait_ge(t["rhoT"], b + 1)
                    if b > 0:
                        dve.wait_ge(a["att"], b)
                    link(nc.vector.tensor_tensor(
                        rho[:], R[:, :].rearrange("p (c q i) -> p c q i", c=C, q=Q4)[:, :, :, 0:QT],
                        mask_f[:, b].unsqueeze(1).broadcast_to([P, C, Q4, QT]), ALU.add))
                    r = rho[:].rearrange("p c q i -> p c (q i)")
                    link(nc.vector.tensor_reduce(rmax[:], r, X, ALU.max))
                    nc.vector.tensor_tensor(r, r, rmax[:].unsqueeze(2).broadcast_to([P, C, TP]),
                                            ALU.subtract).then_inc(v["exp_in"], 1)
                if stage == 2:
                    dve.wait_ge(a["att"], b + 1)
                    for i in range(2):
                        last = nc.vector.tensor_tensor(
                            att[:, 1 + i], att[:, 0],
                            cwcb[:, i, b].rearrange("p q i -> p (q i)").unsqueeze(1)
                            .broadcast_to([P, C, TP]), ALU.mult)
                    link(last)
                    link(nc.vector.tensor_reduce(sums[:].rearrange("p k c -> p (k c)"),
                                                 att[:].rearrange("p k c t -> p (k c) t"), X, ALU.add))
                    link(nc.vector.reciprocal(rden[:], sums[:, 0, :]))
                    nc.vector.tensor_tensor(wsbs_pre[:], sums[:, 1:3, :],
                                            rden[:].unsqueeze(1).broadcast_to([P, 2, C]), ALU.mult)\
                        .then_inc(v["wsbs_pre"], 1)
                if stage == 4:
                    dve.wait_ge(a["wsbs"], b + 1)
                    for c in range(C):
                        last = nc.vector.scalar_tensor_tensor(
                            out=x2[:, c, :], in0=h1[:, b, c, :], scalar=wsbs[:, 0, c:c + 1],
                            in1=x1[:, b, c, :], op0=ALU.mult, op1=ALU.add)
                    link(last)
                    norm_stats(x2)
                if stage == 5:
                    norm_apply(("ffn", b), x2, h2).then_inc(v["h2"], 1)
                if stage == 6:
                    dve.wait_ge(a["h2T"], b + 1)
                    nc.vector.tensor_tensor(h2T_lo[:, b, :], R[:, :], h2T_hi[:, b, :].bitcast(F32),
                                            ALU.subtract).then_inc(v["h2T_lo"], 1)
                if stage == 7:
                    dve.wait_ge(t["gate"], b + 1)
                    link(nc.vector.tensor_tensor(
                        logits[:], R[:, 0:C * E].rearrange("p (c e) -> p c e", c=C),
                        small[:, 0:E].unsqueeze(1).broadcast_to([P, C, E]), ALU.add))
                    for c in range(C):
                        last = nc.vector.max(top[:, c, :], logits[:, c, :])
                    link(last)
                    nc.vector.tensor_tensor(dtop[:], top[:, :, 1], top[:, :, 0], ALU.subtract)\
                        .then_inc(v["dtop"], 1)
                    for c in range(C):
                        last = nc.vector.max_index(top_i[:, c, :], top[:, c, :], logits[:, c, :])
                    link(last)
                    link(nc.vector.tensor_copy(top_f[:], top_i[:]))
                    dve.wait_ge(a["etop"], b + 1)
                    link(nc.vector.tensor_scalar(p2[:], etop[:], 1.0, None, ALU.add))
                    link(nc.vector.reciprocal(p1[:], p2[:]))
                    link(nc.vector.tensor_tensor(p2[:], etop[:], p1[:], ALU.mult))
                    for c in range(C):
                        nc.vector.tensor_scalar(we1[:, c, :], expert_id[:], top_f[:, c, 0:1],
                                                p1[:, c:c + 1], ALU.is_equal, ALU.mult)
                        last = nc.vector.tensor_scalar(we[:, b, c, :], expert_id[:], top_f[:, c, 1:2],
                                                       p2[:, c:c + 1], ALU.is_equal, ALU.mult)
                    link(last)
                    nc.vector.tensor_tensor(we[:, b], we[:, b], we1[:], ALU.add).then_inc(v["we"], 1)
                if stage == 8:
                    dve.wait_ge(t["weT"], b + 1)
                    nc.vector.tensor_copy(weT[:], R[0:E, :]).then_inc(v["weT"], 1)
                if stage == 9:
                    dve.wait_ge(t["b3"], b + 1)
                    for c in range(C):
                        last = nc.vector.scalar_tensor_tensor(
                            out=acc[:, b, c, :], in0=R[:, c * P:(c + 1) * P],
                            scalar=wsbs[:, 1, c:c + 1], in1=x2[:, c, :], op0=ALU.add, op1=ALU.add)
                    last.then_inc(v["acc_start"], 1)
                    dve.wait_ge(v["acc_start"], b + 1)

            def glu(b, e, h):
                n = E * b + e
                for c in range(FC):
                    if positive(FC * (n - 1) + c + 1):
                        dve.wait_ge(v["z_lo"], FC * (n - 1) + c + 1)
                    dve.wait_ge(a["x2b"], FC * n + c + 1)
                    nc.vector.scalar_tensor_tensor(out=z[:, c, :], in0=bank[2 * c][:, :],
                                                   scalar=cols[:, bass.ds(FC * e + c, 1)],
                                                   in1=x2b[:, c, :], op0=ALU.add, op1=ALU.mult)\
                        .then_inc(v["z"], 1)
                for c in range(FC):
                    dve.wait_ge(a["z_hi"], FC * n + c + 1)
                    nc.vector.tensor_tensor(z_lo[:, h, c, :], z[:, c, :], z_hi[:, h, c, :].bitcast(F32),
                                            ALU.subtract).then_inc(v["z_lo"], 1)

            def accumulate(b, e):
                n = E * b + e
                dve.wait_ge(t["y"], n + 1)
                if positive(n):
                    dve.wait_ge(v["acc"], n)
                for c in range(C):
                    last = nc.vector.scalar_tensor_tensor(out=acc[:, b, c, :],
                                                          in0=bank[6][:, c * P:(c + 1) * P],
                                                          scalar=we[:, b, c, bass.ds(e, 1)],
                                                          in1=acc[:, b, c, :], op0=ALU.mult, op1=ALU.add)
                last.then_inc(v["acc"], 1)

            attention(0, 0)
            nc.vector.memset(w_pad[:], 0.0)
            nc.vector.memset(cwcb[:], 0.0)
            link(nc.vector.memset(mask_f[:], PAD))
            full = (QT - 1) * Q4
            dve.wait_ge(mask_in, 16)
            for b in range(B):
                nc.vector.tensor_scalar(mask_f[:, b, :, 0:QT - 1],
                                        mask_i[:, b, 0:full].rearrange("p (i q) -> p q i", q=Q4),
                                        -1.0, 1.0, ALU.mult, ALU.add)
                last = nc.vector.tensor_scalar(mask_f[:, b, 0, QT - 1:QT], mask_i[:, b, full:T],
                                               -1.0, 1.0, ALU.mult, ALU.add)
            link(last)
            for b in range(B):
                nc.vector.tensor_scalar(mask_f[:, b, :, 0:QT - 1], mask_f[:, b, :, 0:QT - 1],
                                        NEG, None, ALU.mult)
                nc.vector.tensor_scalar(mask_f[:, b, 0, QT - 1:QT], mask_f[:, b, 0, QT - 1:QT],
                                        NEG, None, ALU.mult)
            dve.wait_ge(consts_ready, 2)
            nc.vector.tensor_copy(expert_id[:], expert_i[:])
            for stage in range(1, STAGES):
                attention(0, stage)
                if stage == 2:
                    dve.wait_ge(t["cols"], 1)
                    nc.vector.tensor_copy(cols[:], bank[7][:, 0:NROWS])
                    nc.vector.tensor_copy(ctxT[:], bank[7][:, NROWS:NROWS + B * T])
                    nc.vector.tensor_copy(WvT[:], bank[7][:, 256:384]).then_inc(v["cols"], 1)
                if stage == 3:
                    dve.wait_ge(t["WvWo"], 1)
                    nc.vector.tensor_copy(WvWo[:], bank[6][:, 0:P]).then_inc(v["WvWo"], 1)
                if stage == 7:
                    dve.wait_ge(v["cols"], 1)
                    nc.vector.tensor_copy(w_pad[:, QW - 1:QW], cols[:, WX:WX + 1])
                    dve.wait_ge(t["txt"], 1)
                    for b in range(B):
                        for i in range(2):
                            at = (1 + i) * B * T + b * T
                            nc.vector.tensor_copy(
                                cwcb[:, i, b, :, 0:QT - 1],
                                bank[7][:, at:at + full].rearrange("p (i q) -> p q i", q=Q4))
                            nc.vector.tensor_copy(cwcb[:, i, b, 0, QT - 1:QT],
                                                  bank[7][:, at + full:at + T])
                    nc.vector.tensor_copy(txtT[:], bank[7][:, 0:B * T]).then_inc(v["txt"], 1)
            attention(1, 0)
            dve.wait_ge(v["txt"], 1)
            dve.wait_ge(copied["FT"], 1)
            for g in range(AHEAD):
                add_group(g)
            for g in range(GROUPS):
                if g + AHEAD < GROUPS:
                    add_group(g + AHEAD)
                for stage in attention_at[g]:
                    attention(1, stage)
            dve.wait_ge(copied["FT"], 2)
            add_group(GROUPS + 1)
            add_group(GROUPS + 2)
            cross_end(0, 0)
            cross_end(0, 2)
            cross_end(0, 4)
            add_group(GROUPS + 3)
            cross_end(0, 5)
            cross_end(0, 6)
            glu(0, 0, 0)
            cross_end(0, 7)

            def between(place):
                for g in groups_at(place + 1):
                    if on_pool(g) < GROUP:
                        add_group(g)
                for stage in stages_at.get(place, []):
                    cross_end(1, stage)

            for e in range(E):
                between(2 * e)
                glu(*following(0, e), (e + 1) % PAIR)
                if e == 0:
                    cross_end(0, 8)
                    cross_end(0, 9)
                between(2 * e + 1)
                if e:
                    accumulate(0, e - 1)
            between(2 * E)
            glu(1, 1, 1)
            accumulate(0, E - 1)
            with dve.Fori(0, E // PAIR - 1) as pair:
                for h in range(PAIR):
                    glu(1, PAIR * pair + 2 + h, h)
                    accumulate(1, PAIR * pair + h)
            accumulate(1, E - 2)
            dve.wait_ge(v["acc"], B * E - 1)
            for c in range(C):
                dve.wait_ge(t["y_last"], c + 1)
                nc.vector.scalar_tensor_tensor(out=acc[:, B - 1, c, :], in0=bank[c][:, 0:P],
                                               scalar=we[:, B - 1, c, E - 1:E],
                                               in1=acc[:, B - 1, c, :], op0=ALU.mult, op1=ALU.add)\
                    .then_inc(v["acc_last"], 1)


_INS = ["x", "ctx_1024", "mask_BxS2_ik0", "L0_attn_Wq", "L0_attn_Wk", "L0_attn_Wv", "L0_attn_Wo",
        "L0_attn_bo", "L0_attn_gamma", "L0_attn_beta", "L0_xattn_Ws", "L0_xattn_W", "L0_xattn_w",
        "L0_xattn_b", "L0_xattn_Wcw", "L0_xattn_bcw", "L0_xattn_Wcb", "L0_xattn_bcb", "L0_ffn_gate_w",
        "L0_ffn_gate_b", "L0_ffn_w1", "L0_ffn_b1", "L0_ffn_w2", "L0_ffn_b2", "L0_ffn_wg", "L0_ffn_bg",
        "L0_ffn_w3", "L0_ffn_b3"]


def kernel(**inputs):
    import numpy as _np
    import concourse.bacc as _bacc
    from concourse import mybir as _mybir
    from concourse.bass_utils import run_bass_kernel_spmd as _run

    nc = _bacc.Bacc("TRN2", target_bir_lowering=False, num_devices=1)
    arrays, args = {}, []
    for name in _INS:
        a = _np.ascontiguousarray(inputs[name])
        arrays[f"in_{name}_dram"] = a
        args.append(nc.dram_tensor(f"in_{name}_dram", a.shape, _mybir.dt.from_np(a.dtype),
                                   kind="ExternalInput").ap())
    out = nc.dram_tensor("out_dram", inputs["x"].shape, _mybir.dt.float32, kind="ExternalOutput").ap()
    decoder_layer_program(nc, *args, out)
    r = _run(nc, [arrays], core_ids=[0])
    return r.results[0]["out_dram"]
```
